# Optimizing a Trainium2 kernel written in Bass

```python
import numpy as np
import jax
import jax.numpy as jnp

def _softmax(x, axis=-1):
    return jax.nn.softmax(x, axis=axis)

def _gelu(x):
    return jax.nn.gelu(x, approximate=True)

def _silu(x):
    return jax.nn.silu(x)

def _sigmoid(x):
    return jax.nn.sigmoid(x)

def _layernorm(x, axis=-1, eps=1e-05):
    m = jnp.mean(x, axis=axis, keepdims=True)
    v = jnp.var(x, axis=axis, keepdims=True)
    return (x - m) / jnp.sqrt(v + eps)

def _scatter_add(tgt, idx, src, axis=0):
    return tgt.at[idx].add(src)

def _segment_sum(src, seg, n):
    return jax.ops.segment_sum(src, seg, n)
kernel_name = 'mk_adj_resnorm_d2_adj_r2_e02530'

def setup_inputs(seed: int=0):
    np.random.seed(seed)
    _w = jnp.asarray

    def _rec_inputs():
        import jax
        import jax.numpy as jnp
        _gk = jax.random.key(seed)
        x = -0.0001538 + 1 * jax.random.normal(jax.random.fold_in(_gk, 1), (16, 512, 384), jnp.float32)
        _w = (1.0 + jnp.arange(512, dtype=jnp.float32)) ** (-0.5)
        _w = _w / _w.mean()
        _pij = jnp.clip(0.0078125 * _w[:, None] * _w[None, :], 0.0, 1.0)
        _a = jax.random.uniform(jax.random.fold_in(_gk, 2), (16, 512, 512)) < _pij
        _a = jnp.logical_or(_a, jnp.swapaxes(_a, -1, -2))
        _a = jnp.logical_or(_a, jnp.eye(512, dtype=bool))
        _af = _a.astype(jnp.float32)
        _af = _af * jax.random.uniform(jax.random.fold_in(_gk, 3), (16, 512, 512), jnp.float32, 0.05, 4.42607)
        adj = _af
        return (x, adj)
    x, adj = _rec_inputs()

    def _L0_gnn_setup():
        import jax, jax.numpy as jnp
        import numpy as np
        NUM_HEADS = 12
        HIDDEN = 384
        HEAD = HIDDEN // NUM_HEADS
        B, N = (16, 256)
        key = jax.random.key(seed)
        ks = jax.random.split(key, 9)
        s = 0.02
        return {'x': jax.random.normal(ks[0], (B, N, HIDDEN), jnp.float32), 'spatial_encoding': jax.random.normal(ks[1], (B, N, N), jnp.float32), 'edge_encoding': jax.random.normal(ks[2], (B, N, N), jnp.float32), 'Wq': jax.random.normal(ks[3], (HIDDEN, HIDDEN), jnp.float32) * s, 'Wk': jax.random.normal(ks[4], (HIDDEN, HIDDEN), jnp.float32) * s, 'Wv': jax.random.normal(ks[5], (HIDDEN, HIDDEN), jnp.float32) * s, 'bv': jax.random.normal(ks[6], (HIDDEN,), jnp.float32) * s, 'Wo': jax.random.normal(ks[7], (HIDDEN, HIDDEN), jnp.float32) * s, 'bo': jax.random.normal(ks[8], (HIDDEN,), jnp.float32) * s}
    _L0_gnn_all = _L0_gnn_setup()
    _L0_gnn_in = {k: v for k, v in _L0_gnn_all.items() if k in ('Wq', 'Wk', 'Wv', 'bv', 'Wo', 'bo')}
    del _L0_gnn_all

    def _L1_gnn_setup():
        import jax, jax.numpy as jnp
        import numpy as np
        B, N, D, H = (8, 512, 384, 12)
        HD = D // H

        def _split_heads(x):
            b, n, _ = x.shape
            return x.reshape(b, n, H, HD).transpose(0, 2, 1, 3)
        key = jax.random.key(seed)
        ks = jax.random.split(key, 10)
        input_graph = jax.random.normal(ks[0], (B, N, D), dtype=jnp.float32)
        u = jax.random.uniform(ks[1], (B, N, N), dtype=jnp.float32)
        keep = jax.random.uniform(ks[2], (B, N, N)) < 0.15
        adj = jnp.where(keep, u, 0.0)
        s = 1.0 / np.sqrt(D)
        Wq = jax.random.normal(ks[3], (D, D), dtype=jnp.float32) * s
        bq = jnp.zeros((D,), dtype=jnp.float32)
        Wk = jax.random.normal(ks[4], (D, D), dtype=jnp.float32) * s
        bk = jnp.zeros((D,), dtype=jnp.float32)
        Wv = jax.random.normal(ks[5], (D, D), dtype=jnp.float32) * s
        bv = jnp.zeros((D,), dtype=jnp.float32)
        beta = jnp.asarray(0.1, dtype=jnp.float32)
        return {'input_graph': input_graph, 'adj': adj, 'Wq': Wq, 'bq': bq, 'Wk': Wk, 'bk': bk, 'Wv': Wv, 'bv': bv, 'beta': beta}
    _L1_gnn_all = _L1_gnn_setup()
    _L1_gnn_in = {k: v for k, v in _L1_gnn_all.items() if k in ('Wq', 'bq', 'Wk', 'bk', 'Wv', 'bv', 'beta')}
    del _L1_gnn_all
    return {'x': x, 'adj': adj, 'L0_gnn_Wq': _L0_gnn_in['Wq'], 'L0_gnn_Wk': _L0_gnn_in['Wk'], 'L0_gnn_Wv': _L0_gnn_in['Wv'], 'L0_gnn_bv': _L0_gnn_in['bv'], 'L0_gnn_Wo': _L0_gnn_in['Wo'], 'L0_gnn_bo': _L0_gnn_in['bo'], 'L1_gnn_Wq': _L1_gnn_in['Wq'], 'L1_gnn_bq': _L1_gnn_in['bq'], 'L1_gnn_Wk': _L1_gnn_in['Wk'], 'L1_gnn_bk': _L1_gnn_in['bk'], 'L1_gnn_Wv': _L1_gnn_in['Wv'], 'L1_gnn_bv': _L1_gnn_in['bv'], 'L1_gnn_beta': _L1_gnn_in['beta']}

def reference(x, adj, L0_gnn_Wq, L0_gnn_Wk, L0_gnn_Wv, L0_gnn_bv, L0_gnn_Wo, L0_gnn_bo, L1_gnn_Wq, L1_gnn_bq, L1_gnn_Wk, L1_gnn_bk, L1_gnn_Wv, L1_gnn_bv, L1_gnn_beta):
    import jax
    import jax.numpy as jnp

    def _L0_gnn_ref(x, spatial_encoding, edge_encoding, Wq, Wk, Wv, bv, Wo, bo):
        import jax, jax.numpy as jnp
        import numpy as np
        NUM_HEADS = 12
        HIDDEN = 384
        HEAD = HIDDEN // NUM_HEADS
        B, N = (16, 256)
        b, n, h = x.shape
        scale = jnp.asarray(HIDDEN, x.dtype) ** (-0.5)
        q = (x @ Wq.T).reshape(b, n, NUM_HEADS, HEAD)
        k = (x @ Wk.T).reshape(b, n, NUM_HEADS, HEAD)
        v = (x @ Wv.T + bv).reshape(b, n, NUM_HEADS, HEAD)
        bias = (spatial_encoding + edge_encoding)[:, None]
        scores = jnp.einsum('bqhd,bkhd->bhqk', q, k) * scale + bias
        row_nonzero = jnp.any(scores != 0, axis=-1, keepdims=True)
        scores = jnp.where(row_nonzero, scores, -jnp.inf)
        p = jax.nn.softmax(scores, axis=-1)
        p = jnp.nan_to_num(p)
        out = jnp.einsum('bhqk,bkhd->bqhd', p, v).reshape(b, n, h)
        return out @ Wo.T + bo

    def _L1_gnn_ref(input_graph, adj, Wq, bq, Wk, bk, Wv, bv, beta):
        import jax, jax.numpy as jnp
        import numpy as np
        B, N, D, H = (8, 512, 384, 12)
        HD = D // H

        def _split_heads(x):
            b, n, _ = x.shape
            return x.reshape(b, n, H, HD).transpose(0, 2, 1, 3)
        q = _split_heads(input_graph @ Wq + bq)
        k = _split_heads(input_graph @ Wk + bk)
        v = _split_heads(input_graph @ Wv + bv)
        scores = jnp.einsum('bhqd,bhkd->bhqk', q, k) / jnp.sqrt(jnp.asarray(HD, input_graph.dtype))
        adj_e = adj[:, None, :, :]
        scores = scores + beta * adj_e
        scores = jnp.where(adj_e > 0, scores, jnp.asarray(-9000000000000000.0, scores.dtype))
        probs = jax.nn.softmax(scores, axis=-1)
        out = jnp.einsum('bhqk,bhkd->bhqd', probs, v)
        return out.transpose(0, 2, 1, 3).reshape(input_graph.shape[0], input_graph.shape[1], D)
    x = _layernorm(x + _L0_gnn_ref(x, adj, adj, L0_gnn_Wq, L0_gnn_Wk, L0_gnn_Wv, L0_gnn_bv, L0_gnn_Wo, L0_gnn_bo), axis=-1)
    x = _layernorm(x + _L1_gnn_ref(x, adj, L1_gnn_Wq, L1_gnn_bq, L1_gnn_Wk, L1_gnn_bk, L1_gnn_Wv, L1_gnn_bv, L1_gnn_beta), axis=-1)
    return x

_drawn_inputs = setup_inputs


def setup_inputs(seed=0):
    import zlib

    import numpy as np

    out = dict(_drawn_inputs(seed))
    spreads = {'L1_gnn_bq': (0.0, 0.1), 'L1_gnn_bk': (0.0, 0.8), 'L1_gnn_bv': (0.0, 0.1)}
    factors = {'L0_gnn_Wq': 8.0, 'L0_gnn_Wk': 8.0, 'L0_gnn_bv': 4.922}
    for name, (base, spread) in spreads.items():
        noise = np.random.default_rng([zlib.crc32(name.encode()), seed]).standard_normal(out[name].shape)
        drawn = base * np.exp(spread * noise) if base else spread * noise
        out[name] = jnp.asarray(drawn.astype(out[name].dtype))
    for name, factor in factors.items():
        out[name] = (out[name] * factor).astype(out[name].dtype)
    return out
```

```python
from contextlib import ExitStack

import concourse.bass as bass
from concourse import mybir

F32 = mybir.dt.float32
F32R = mybir.dt.float32r
ALU = mybir.AluOpType
ACT = mybir.ActivationFunctionType

P = 128
B, N, D, H = 16, 512, 384, 12
HD = D // H
GH = P // HD
G = H // GH
C = N // P
HALF = N // 2
BLOCKS = 2 * G
PAIRS = GH * BLOCKS
AHEAD = 2
STACK = 3 * HD
RING = 3
MASKED = -9000000000000000.0
LN_EPS = 1e-5
BIG = 3.0e38
DMA = 16

JOBS = {0: ("q", "own", 2), 1: ("k", "own", 2), 2: ("v", "own", 2),
        3: ("n", "post", 0), 4: ("n", "post", 1), 5: ("n", "post", 2), 6: ("n", "post", 3),
        7: ("b", "post", 0), 8: ("b", "post", 1), 9: ("b", "post", 2),
        10: ("w", "post", 0), 11: ("w", "post", 1), 12: ("w", "post", 2), 13: ("w", "post", 3),
        14: ("x", "next", 0), 15: ("x", "next", 1), 16: ("x", "next", 2),
        17: ("q", "next", 0), 18: ("k", "next", 0), 19: ("v", "next", 0),
        20: ("q", "next", 1), 21: ("k", "next", 1), 22: ("v", "next", 1)}
FIRST_JOBS = [("x", 0), ("x", 1), ("x", 2), ("q", 0), ("k", 0), ("v", 0), ("q", 1), ("k", 1), ("v", 1)]
ON_ACT = [p % 2 == 0 or p in (5, 13, 21) for p in range(PAIRS)]


class Unit:

    def __init__(self, layer, graph):
        self.layer, self.graph = layer, graph

    def before(self):
        if self.layer and isinstance(self.graph, int) and self.graph == 0:
            return Unit(0, B - 1)
        return Unit(self.layer, self.graph - 1)


class Signal:

    def __init__(self, sem, layer0, layer1=None):
        self.sem = sem
        self.per = (layer0, layer0 if layer1 is None else layer1)

    def at(self, unit, count):
        return unit.graph * self.per[unit.layer] + (unit.layer * B * self.per[0] + count)

    def begun(self, unit, count):
        value = self.at(unit, count)
        return not isinstance(value, int) or value > 0


def place(p):
    block = p // GH
    return block, block // 2, block % 2, p % GH


def two_layer_graph_attention(nc, x, adj, wq0, wk0, wv0, bv0, wo0, bo0,
                              wq1, bq1, wk1, bk1, wv1, bv1, beta, out):
    with ExitStack() as ctx:
        def sb(name, shape, dt=F32):
            return ctx.enter_context(nc.sbuf_tensor(name, [P] + shape, dt))

        def signal(name, layer0=1, layer1=None):
            return Signal(ctx.enter_context(nc.semaphore(name)), layer0, layer1)

        x1 = nc.dram_tensor("x1_scratch", [B, N, D], F32, kind="Internal").ap()

        ident = sb("ident", [P])
        w_raw = sb("w_raw", [G, D])
        w_hi = sb("w_hi", [3, G, D], F32R)
        w_lo = sb("w_lo", [3, G, D], F32R)
        wo_hi = sb("wo_hi", [G, D], F32R)
        wo_lo = sb("wo_lo", [G, D], F32R)
        bq_col = sb("bq_col", [G])
        bk_col = sb("bk_col", [G])
        bv_row = sb("bv_row", [2, D])
        bo_row = sb("bo_row", [D])
        beta_col = sb("beta_col", [1])
        pow_col = sb("pow_col", [C])
        adj_raw = sb("adj_raw", [C, N])
        bias = sb("bias", [C, N])
        x_in = sb("x_in", [C, D])
        att = x_in
        x_res = sb("x_res", [C, D])
        xT_hi = sb("xT_hi", [G, N], F32R)
        xT_lo = sb("xT_lo", [G, N], F32R)
        q_hi, q_lo = sb("q_hi", [N], F32R), sb("q_lo", [N], F32R)
        k_hi, k_lo = sb("k_hi", [N], F32R), sb("k_lo", [N], F32R)
        q_stack = sb("q_stack", [H, N], F32R)
        k_stack = sb("k_stack", [H, N], F32R)
        v_sb = sb("v_sb", [G, C, P])
        minus_s = sb("minus_s", [2, 2, N])
        probs = sb("probs", [2, 2, N])
        probsT = sb("probsT", [2, GH, C, HALF])
        minus_max = sb("minus_max", [RING, 2, GH])
        sums = sb("sums", [RING, 2, GH])
        zero_row = sb("zero_row", [2, GH])
        rinv = sb("rinv", [C, H])
        oT = sb("oT", [G, N])
        stats = sb("stats", [C, 6])
        mean_var = sb("mean_var", [C, 2])
        var_eps = sb("var_eps", [C])
        rstd = sb("rstd", [C])

        ps_s = ctx.enter_context(nc.psum_tensor("ps_s", [P, 2, N], F32))
        ps_t = ctx.enter_context(nc.psum_tensor("ps_t", [P, 2, 2, C, P], F32))
        ps_o = ctx.enter_context(nc.psum_tensor("ps_o", [P, N], F32))
        ps_job = ctx.enter_context(nc.psum_tensor("ps_job", [P, N], F32))

        setup_loaded = signal("setup_loaded")
        setup_pool = signal("setup_pool")
        setup_scaled = signal("setup_scaled")
        w_loaded = signal("w_loaded")
        w_hi_out, w_lo_out = signal("w_hi_out"), signal("w_lo_out")
        raw_loaded = [signal(f"raw_loaded{i}", DMA) for i in range(2)]
        xin_loaded = signal("xin_loaded", DMA)
        xres_loaded = signal("xres_loaded", DMA)
        stored = signal("stored", DMA)
        q_stacked = [signal(f"q_stacked{g}", 3 * GH * DMA) for g in range(G)]
        k_stacked = [signal(f"k_stacked{g}", 3 * GH * DMA) for g in range(G)]
        scored = signal("scored", 2 * PAIRS)
        maxed = signal("maxed", 2 * PAIRS)
        expd = signal("expd", 2 * PAIRS)
        turned = signal("turned", PAIRS)
        turned_out_act = signal("turned_out_act", sum(ON_ACT))
        turned_out_dve = signal("turned_out_dve", PAIRS - sum(ON_ACT))
        o_ready, o_out = signal("o_ready", BLOCKS), signal("o_out", BLOCKS)
        per_job = {"x": (G, G), "q": (G, G), "k": (G, G), "v": (G, G), "n": (C, C), "b": (G, 0), "w": (C, 0)}
        job_ready = {j: signal(f"{j}_ready", *n) for j, n in per_job.items()}
        job_hi = {j: signal(f"{j}_hi_out", *per_job[j]) for j in "xqkb"}
        summed = signal("summed", C)
        job_out = {j: signal(f"{j}_out", *per_job[j]) for j in "xqkvnb"} | {"w": summed}
        inverted = signal("inverted", BLOCKS)
        inverting = signal("inverting", 4 * BLOCKS, BLOCKS)
        bias_masked = signal("bias_masked", 0, 2)
        bias_out = signal("bias_out", 2)
        stats_out = signal("stats_out", C)
        mean_out = signal("mean_out", C)
        var_out = signal("var_out", 1)
        rstd_out = signal("rstd_out", 1)
        normed = signal("normed", 1)
        bo_added = signal("bo_added", 1, 0)
        waits_carried = signal("waits_carried")

        def nodes(t, unit):
            return t[unit.graph].rearrange("(c p) d -> p c d", p=P)

        def turned_out(p):
            act = sum(ON_ACT[:p % PAIRS + 1]) + p // PAIRS * sum(ON_ACT)
            return (turned_out_act, act) if ON_ACT[p] else (turned_out_dve, p + 1 - act)

        def job_at(step, own, post, nxt):
            kind, whose, i = JOBS.get(step, (None, None, None))
            unit = {"own": own, "post": post, "next": nxt, None: None}[whose]
            if unit is None or (kind in "bw" and unit.layer):
                return None
            return kind, unit, i

        def units(eng, body):
            body(Unit(0, 0), None, Unit(0, 1))
            with eng.Fori(1, B - 1) as graph:
                body(Unit(0, graph), Unit(0, graph - 1), Unit(0, graph + 1))
            body(Unit(0, B - 1), Unit(0, B - 2), Unit(1, 0))
            body(Unit(1, 0), Unit(0, B - 1), Unit(1, 1))
            with eng.Fori(1, B - 1) as graph:
                body(Unit(1, graph), Unit(1, graph - 1), Unit(1, graph + 1))
            body(Unit(1, B - 1), Unit(1, B - 2), None)

        LAST = Unit(1, B - 1)
        weights = [(wq0, 0), (wk0, 1), (wv0, 2), (wo0, None), (wq1, 0), (wk1, 1), (wv1, 2)]
        scale = {0: float(D) ** -0.5, 4: float(HD) ** -0.5}

        block = ctx.enter_context(nc.Block())

        @block.sync
        def _(sp):
            def load_weight(i):
                if i:
                    sp.wait_ge(w_lo_out.sem, i)
                sp.dma_start(w_raw[:], weights[i][0].rearrange("(t p) n -> p t n", p=P)).then_inc(w_loaded.sem, DMA)

            def load_adj(unit, half):
                sp.wait_ge(bias_out.sem, bias_out.at(unit, half - 1))
                rows = slice(2 * half, 2 * half + 2)
                sp.dma_start(adj_raw[:, rows, :], nodes(adj, unit)[:, rows, :]).then_inc(raw_loaded[half].sem, DMA)

            def load_xin(unit, own, post):
                source = x1 if unit.layer else x
                if own is not None:
                    sp.wait_ge(job_ready["x"].sem, job_ready["x"].at(own, G))
                if post is not None and post.layer == 0:
                    sp.wait_ge(job_ready["b"].sem, job_ready["b"].at(post, G))
                elif post is not None:
                    sp.wait_ge(summed.sem, summed.at(post, C))
                sp.dma_start(x_in[:], nodes(source, unit)).then_inc(xin_loaded.sem, DMA)

            def load_xres(unit):
                sp.dma_start(x_res[:], nodes(x1 if unit.layer else x, unit)).then_inc(xres_loaded.sem, DMA)

            def store(post):
                sp.wait_ge(normed.sem, normed.at(post, 1))
                target = out if post.layer else x1
                sp.dma_start(nodes(target, post), x_res[:]).then_inc(stored.sem, DMA)
                sp.wait_ge(stored.sem, stored.at(post, DMA))

            def stack(unit, g):
                for kind, stacked, to, hi, lo, rows in (("q", q_stacked, q_stack, q_hi, q_lo, (0, 2, 1)),
                                                        ("k", k_stacked, k_stack, k_hi, k_lo, (0, 1, 2))):
                    sp.wait_ge(job_hi[kind].sem, job_hi[kind].at(unit, g + 1))
                    for n, (src, row) in enumerate(zip((hi, hi, lo), rows)):
                        if n == 2:
                            sp.wait_ge(job_out[kind].sem, job_out[kind].at(unit, g + 1))
                        for h in range(GH):
                            sp.dma_start(to[HD * row:HD * row + HD, GH * g + h, :].bitcast(F32),
                                         src[HD * h:HD * h + HD, :].bitcast(F32)).then_inc(stacked[g].sem, DMA)

            def unit(own, post, nxt):
                stack(own, 2)
                if nxt is not None:
                    load_adj(nxt, 0)
                    load_adj(nxt, 1)
                    if nxt.layer != own.layer:
                        for i in range(4, 7):
                            load_weight(i)
                    load_xin(nxt, own, post)
                if post is not None:
                    store(post)
                    load_xres(own)
                if nxt is not None:
                    stack(nxt, 0)
                    stack(nxt, 1)

            first = Unit(0, 0)
            load_xin(first, None, None)
            load_weight(0)
            sp.dma_start(bv_row[:, 0, :], bv0.partition_broadcast(P)).then_inc(setup_loaded.sem, DMA)
            sp.dma_start(bv_row[:, 1, :], bv1.partition_broadcast(P)).then_inc(setup_loaded.sem, DMA)
            sp.dma_start(bo_row[:], bo0.partition_broadcast(P)).then_inc(setup_loaded.sem, DMA)
            sp.dma_start(beta_col[:], beta.partition_broadcast(P)).then_inc(setup_loaded.sem, DMA)
            sp.dma_start(bq_col[:], bq1.rearrange("(g p) -> p g", p=P),
                         allow_slow_non_contiguous=True).then_inc(setup_loaded.sem, DMA)
            sp.dma_start(bk_col[:], bk1.rearrange("(g p) -> p g", p=P),
                         allow_slow_non_contiguous=True).then_inc(setup_loaded.sem, DMA)
            for half in range(2):
                rows = slice(2 * half, 2 * half + 2)
                sp.dma_start(adj_raw[:, rows, :], nodes(adj, first)[:, rows, :]).then_inc(raw_loaded[half].sem, DMA)
            for i in range(1, 4):
                load_weight(i)
            load_xres(first)
            stack(first, 0)
            stack(first, 1)
            units(sp, unit)
            store(LAST)

        @block.gpsimd
        def _(pool):
            pool.memset(ident[:], 0.0).then_inc(setup_pool.sem, 1)
            pool.memset(pow_col[:], -0.5).then_inc(setup_pool.sem, 1)
            pool.wait_ge(setup_pool.sem, 2)
            pool.affine_select(out=ident[:], in_=ident[:], compare_op=ALU.not_equal, fill=1.0, base=0,
                               pattern=[[-1, P]], channel_multiplier=1).then_inc(setup_pool.sem, 1)

            def post_stage(post):
                if post.layer == 0:
                    pool.wait_ge(xres_loaded.sem, xres_loaded.at(post, DMA))
                    pool.tensor_tensor(x_res[:], x_res[:], bo_row[:, None, :].to_broadcast([P, C, D]),
                                       ALU.add).then_inc(bo_added.sem, 1)
                pool.wait_ge(var_out.sem, var_out.at(post, 1))
                pool.tensor_tensor(rstd[:], var_eps[:], pow_col[:], ALU.pow).then_inc(rstd_out.sem, 1)

            pool.wait_ge(setup_loaded.sem, 6 * DMA)
            units(pool, lambda own, post, nxt: post is not None and post_stage(post))
            post_stage(LAST)

        @block.tensor
        def _(pe):
            def products(ps, a, b):
                for n, (s, m) in enumerate(((a[0], b[0]), (a[0], b[1]), (a[1], b[0]))):
                    for t in range(G):
                        mm = pe.matmul(ps, s(t), m(t), start=(n == 0 and t == 0), stop=(n == 2 and t == G - 1))
                return mm

            def cols(tile, *at):
                lead, (a, b) = at[:-1], at[-1]
                return lambda t: tile[(slice(None), *lead, t, slice(a, b))]

            def job(kind, unit, i):
                w = w_hi, w_lo
                xT = xT_hi, xT_lo
                if kind == "x":
                    if i == 0:
                        pe.wait_ge(xin_loaded.sem, xin_loaded.at(unit, DMA))
                    for c in range(C):
                        mm = pe.transpose(ps_job[:, P * c:P * c + P], x_in[:, c, P * i:P * i + P], ident[:])
                elif kind in "qk":
                    m = "qk".index(kind)
                    pe.wait_ge(job_out["x"].sem, job_out["x"].at(unit, G))
                    pe.wait_ge(w_lo_out.sem, 7 if unit.layer else 3)
                    mm = products(ps_job[:], [cols(t, m, (P * i, P * i + P)) for t in w],
                                  [cols(t, (0, N)) for t in xT])
                elif kind == "v":
                    for c in range(C):
                        mm = products(ps_job[:, P * c:P * c + P], [cols(t, (P * c, P * c + P)) for t in xT],
                                      [cols(t, 2, (P * i, P * i + P)) for t in w])
                elif kind == "n":
                    if i == 0:
                        pe.wait_ge(o_out.sem, o_out.at(unit, BLOCKS))
                    for g in range(G):
                        mm = pe.transpose(ps_job[:, P * g:P * g + P], oT[:, g, P * i:P * i + P], ident[:])
                elif kind == "b":
                    if i == 0:
                        pe.wait_ge(job_out["n"].sem, job_out["n"].at(unit, C))
                    for c in range(C):
                        mm = pe.transpose(ps_job[:, P * c:P * c + P], att[:, c, P * i:P * i + P], ident[:])
                elif kind == "w":
                    if i == 0:
                        pe.wait_ge(job_out["b"].sem, job_out["b"].at(unit, G))
                        pe.wait_ge(w_lo_out.sem, 4)
                    mm = products(ps_job[:, 0:D], [cols(t, (P * i, P * i + P)) for t in xT],
                                  [cols(t, (0, D)) for t in (wo_hi, wo_lo)])
                mm.then_inc(job_ready[kind].sem, 1)

            previous = [None]

            def side_job(todo):
                if todo is None:
                    return
                if previous[0] is not None:
                    kind, unit, i = previous[0]
                    pe.wait_ge(job_out[kind].sem, job_out[kind].at(unit, i + 1))
                job(*todo)
                previous[0] = todo

            def score(unit, p):
                _, g, half, h = place(p)
                if p % (2 * GH) == 0:
                    pe.wait_ge(q_stacked[g].sem, q_stacked[g].at(unit, 3 * GH * DMA))
                    pe.wait_ge(k_stacked[g].sem, k_stacked[g].at(unit, 3 * GH * DMA))
                for c in range(2):
                    if maxed.begun(unit, 2 * p + c - 1):
                        pe.wait_ge(maxed.sem, maxed.at(unit, 2 * p + c - 1))
                    q0 = P * (2 * half + c)
                    pe.matmul(ps_s[:, c, :], q_stack[0:STACK, GH * g + h, q0:q0 + P],
                              k_stack[0:STACK, GH * g + h, :], start=True, stop=True).then_inc(scored.sem, 1)

            def turn(unit, p):
                out_of_banks, count = turned_out(p - 2)
                if out_of_banks.begun(unit, count):
                    pe.wait_ge(out_of_banks.sem, out_of_banks.at(unit, count))
                for c in range(2):
                    pe.wait_ge(expd.sem, expd.at(unit, 2 * p + c + 1))
                    for kc in range(C):
                        mm = pe.transpose(ps_t[:, p % 2, c, kc, :], probs[:, p % 2, c, P * kc:P * kc + P], ident[:])
                mm.then_inc(turned.sem, 1)

            def weigh_values(unit, b):
                g, half = b // 2, b % 2
                if half == 0:
                    pe.wait_ge(job_out["v"].sem, job_out["v"].at(unit, g + 1))
                for p in (GH * b + GH - 2, GH * b + GH - 1):
                    in_sbuf, count = turned_out(p)
                    pe.wait_ge(in_sbuf.sem, in_sbuf.at(unit, count))
                if o_out.begun(unit, b):
                    pe.wait_ge(o_out.sem, o_out.at(unit, b))
                for kc in range(C):
                    for h in range(GH):
                        mm = pe.matmul(ps_o[HD * h:HD * h + HD, HALF * half:HALF * half + HALF],
                                       v_sb[:, g, kc, HD * h:HD * h + HD], probsT[:, b % 2, h, kc, :],
                                       start=(kc == 0), stop=(kc == C - 1))
                mm.then_inc(o_ready.sem, 1)

            def unit(own, post, nxt):
                previous[0] = ("v", own, 1)
                for p in range(PAIRS):
                    ahead = p + AHEAD
                    if ahead < PAIRS:
                        score(own, ahead)
                    elif nxt is not None:
                        score(nxt, ahead - PAIRS)
                    turn(own, p)
                    if p % GH == 1 and p > GH:
                        weigh_values(own, p // GH - 1)
                    elif p == 1 and post is not None:
                        weigh_values(post, BLOCKS - 1)
                    side_job(job_at(p, own, post, nxt))

            pe.wait_ge(setup_pool.sem, 3)
            for kind, i in FIRST_JOBS:
                side_job((kind, Unit(0, 0), i))
            for p in range(AHEAD):
                score(Unit(0, 0), p)
            units(pe, unit)
            weigh_values(LAST, BLOCKS - 1)
            previous[0] = None
            for i in range(C):
                side_job(("n", LAST, i))

        @block.scalar
        def _(act):
            def split_weight(i):
                m = weights[i][1]
                act.wait_ge(w_loaded.sem, DMA * (i + 1))
                if i == 4:
                    act.wait_ge(job_ready["v"].sem, job_ready["v"].at(Unit(0, B - 1), G))
                hi = wo_hi[:] if m is None else w_hi[:, m]
                act.activation(hi, w_raw[:], ACT.Copy, scale=scale.get(i, 1.0)).then_inc(w_hi_out.sem, 1)

            def job(kind, unit, i):
                if kind not in job_hi:
                    return
                act.wait_ge(job_ready[kind].sem, job_ready[kind].at(unit, i + 1))
                if kind in "qk":
                    stacked = q_stacked if kind == "q" else k_stacked
                    before, g = (unit, i - 1) if i else (unit.before(), G - 1)
                    if stacked[g].begun(before, 3 * GH * DMA):
                        act.wait_ge(stacked[g].sem, stacked[g].at(before, 3 * GH * DMA))
                to = {"x": xT_hi[:, i, :], "b": xT_hi[:, i, :], "q": q_hi[:], "k": k_hi[:]}[kind]
                if kind in "qk" and unit.layer:
                    col = (bq_col if kind == "q" else bk_col)[:, i:i + 1]
                    done = act.activation(to, ps_job[:], ACT.Identity, bias=col)
                else:
                    done = act.activation(to, ps_job[:], ACT.Copy)
                done.then_inc(job_hi[kind].sem, 1)

            def exponentials(unit, p):
                b, _, _, h = place(p)
                if p % GH == 0:
                    if inverted.begun(unit, b - RING + 1):
                        act.wait_ge(inverted.sem, inverted.at(unit, b - RING + 1))
                if turned.begun(unit, p - 1):
                    act.wait_ge(turned.sem, turned.at(unit, p - 1))
                for c in range(2):
                    act.wait_ge(maxed.sem, maxed.at(unit, 2 * p + c + 1))
                    act.activation(probs[:, p % 2, c, :], minus_s[:, p % 2, c, :], ACT.Exp,
                                   bias=minus_max[:, b % RING, c, h:h + 1], scale=-1.0,
                                   accum_out=sums[:, b % RING, c, h:h + 1]).then_inc(expd.sem, 1)

            def turned_copy(unit, p):
                b, _, _, h = place(p)
                if p % GH == 0:
                    if o_ready.begun(unit, b - 1):
                        act.wait_ge(o_ready.sem, o_ready.at(unit, b - 1))
                act.wait_ge(turned.sem, turned.at(unit, p + 1))
                act.activation(probsT[:, b % 2, h].rearrange("p k (c q) -> p c k q", c=2), ps_t[:, p % 2],
                               ACT.Copy).then_inc(turned_out_act.sem, 1)

            def o_copy(unit, b):
                g, half = b // 2, b % 2
                act.wait_ge(o_ready.sem, o_ready.at(unit, b + 1))
                if g == 0:
                    if job_ready["n"].begun(unit.before(), 2 * half + 2):
                        act.wait_ge(job_ready["n"].sem, job_ready["n"].at(unit.before(), 2 * half + 2))
                cols = slice(HALF * half, HALF * half + HALF)
                act.activation(oT[:, g, cols], ps_o[:, cols], ACT.Copy).then_inc(o_out.sem, 1)

            def unit(own, post, nxt):
                for p in range(PAIRS):
                    ahead = p + AHEAD
                    if ahead < PAIRS:
                        exponentials(own, ahead)
                    elif nxt is not None:
                        exponentials(nxt, ahead - PAIRS)
                    if ON_ACT[p]:
                        turned_copy(own, p)
                    if p % GH == 1 and p > GH:
                        o_copy(own, p // GH - 1)
                    elif p == 1 and post is not None:
                        o_copy(post, BLOCKS - 1)
                    todo = job_at(p, own, post, nxt)
                    if todo is not None:
                        job(*todo)
                    if nxt is not None and nxt.layer != own.layer and p in (5, 7, 9):
                        split_weight(4 + (p - 5) // 2)

            for i in range(4):
                split_weight(i)
            act.wait_ge(setup_scaled.sem, 1)
            for kind, i in FIRST_JOBS:
                job(kind, Unit(0, 0), i)
            for p in range(AHEAD):
                exponentials(Unit(0, 0), p)
            units(act, unit)
            o_copy(LAST, BLOCKS - 1)

        @block.vector
        def _(dve):
            def carry_wait():
                dve.sem_inc(waits_carried.sem, 1)

            def split_weight(i):
                m = weights[i][1]
                dve.wait_ge(w_hi_out.sem, i + 1)
                hi, lo = (wo_hi[:], wo_lo[:]) if m is None else (w_hi[:, m], w_lo[:, m])
                flat = "p t n -> p (t n)"
                dve.scalar_tensor_tensor(lo.rearrange(flat), w_raw[:].rearrange(flat), scale.get(i, 1.0),
                                         hi.bitcast(F32).rearrange(flat), ALU.mult,
                                         ALU.subtract).then_inc(w_lo_out.sem, 1)

            def make_bias(unit, half):
                rows = slice(2 * half, 2 * half + 2)
                raw, to = adj_raw[:, rows, :], bias[:, rows, :]
                dve.wait_ge(raw_loaded[half].sem, raw_loaded[half].at(unit, DMA))
                if unit.layer == 0:
                    dve.tensor_scalar(to, raw, 2.0, None, ALU.mult).then_inc(bias_out.sem, 1)
                else:
                    dve.tensor_scalar(to, raw, 0.0, MASKED, ALU.is_le, ALU.mult).then_inc(bias_masked.sem, 1)
                    dve.wait_ge(bias_masked.sem, bias_masked.at(unit, half + 1))
                    dve.scalar_tensor_tensor(to, raw, beta_col[:, 0:1], to, ALU.mult,
                                             ALU.add).then_inc(bias_out.sem, 1)

            def maxima(unit, p):
                b, g, half, h = place(p)
                if p % GH == 0 and g == 0:
                    dve.wait_ge(bias_out.sem, bias_out.at(unit, half + 1))
                if expd.begun(unit, 2 * p - 2):
                    dve.wait_ge(expd.sem, expd.at(unit, 2 * p - 2))
                for c in range(2):
                    dve.wait_ge(scored.sem, scored.at(unit, 2 * p + c + 1))
                    carry_wait()
                    dve.tensor_tensor_reduce(minus_s[:, p % 2, c, :], ps_s[:, c, :], bias[:, 2 * half + c, :],
                                             -1.0, BIG, ALU.add, ALU.min,
                                             minus_max[:, b % RING, c, h:h + 1]).then_inc(maxed.sem, 1)

            def invert(unit, b):
                g, half = b // 2, b % 2
                to = rinv[:, 2 * half:2 * half + 2, GH * g:GH * g + GH]
                dve.wait_ge(expd.sem, expd.at(unit, 2 * GH * (b + 1)))
                s, m = sums[:, b % RING], minus_max[:, b % RING]
                if unit.layer:
                    dve.reciprocal(to, s).then_inc(inverted.sem, 1)
                    return
                dve.reciprocal(to, s).then_inc(inverting.sem, 1)
                dve.tensor_scalar(zero_row[:], s, float(N), None, ALU.is_equal).then_inc(inverting.sem, 1)
                dve.wait_ge(inverting.sem, inverting.at(unit, 4 * b + 2))
                dve.scalar_tensor_tensor(zero_row[:], m, 0.0, zero_row[:], ALU.is_equal,
                                         ALU.mult).then_inc(inverting.sem, 1)
                dve.wait_ge(inverting.sem, inverting.at(unit, 4 * b + 3))
                dve.tensor_scalar(zero_row[:], zero_row[:], -1.0, 1.0, ALU.mult, ALU.add).then_inc(inverting.sem, 1)
                dve.wait_ge(inverting.sem, inverting.at(unit, 4 * b + 4))
                dve.tensor_tensor(to, to, zero_row[:], ALU.mult).then_inc(inverted.sem, 1)

            def turned_copy(unit, p):
                b, _, _, h = place(p)
                if p % GH in (0, 1):
                    if o_ready.begun(unit, b - 1):
                        dve.wait_ge(o_ready.sem, o_ready.at(unit, b - 1))
                dve.wait_ge(turned.sem, turned.at(unit, p + 1))
                dve.tensor_copy(probsT[:, b % 2, h].rearrange("p k (c q) -> p c k q", c=2),
                                ps_t[:, p % 2]).then_inc(turned_out_dve.sem, 1)

            def row_stats(unit, c):
                dve.wait_ge(summed.sem, summed.at(unit, c + 1))
                dve.bn_stats(stats[:, c, :], x_res[:, c, :]).then_inc(stats_out.sem, 1)

            def job(kind, unit, i):
                if kind in job_hi:
                    dve.wait_ge(job_hi[kind].sem, job_hi[kind].at(unit, i + 1))
                    hi, lo = {"x": (xT_hi[:, i, :], xT_lo[:, i, :]), "b": (xT_hi[:, i, :], xT_lo[:, i, :]),
                              "q": (q_hi[:], q_lo[:]), "k": (k_hi[:], k_lo[:])}[kind]
                    if kind in "qk" and unit.layer:
                        col = (bq_col if kind == "q" else bk_col)[:, i:i + 1]
                        done = dve.scalar_tensor_tensor(lo, ps_job[:], col, hi.bitcast(F32), ALU.add, ALU.subtract)
                    else:
                        done = dve.tensor_tensor(lo, ps_job[:], hi.bitcast(F32), ALU.subtract)
                    done.then_inc(job_out[kind].sem, 1)
                    return
                dve.wait_ge(job_ready[kind].sem, job_ready[kind].at(unit, i + 1))
                if kind == "v":
                    row = bv_row[:, unit.layer, None, P * i:P * i + P].to_broadcast([P, C, P])
                    dve.tensor_tensor(v_sb[:, i], ps_job[:].rearrange("p (c d) -> p c d", c=C), row,
                                      ALU.add).then_inc(job_out["v"].sem, 1)
                elif kind == "n":
                    if i == 0:
                        dve.wait_ge(inverted.sem, inverted.at(unit, BLOCKS))
                    dve.tensor_tensor(att[:, i, :].rearrange("p (h d) -> p h d", h=H),
                                      ps_job[:, 0:D].rearrange("p (h d) -> p h d", h=H),
                                      rinv[:, i, :, None].to_broadcast([P, H, HD]),
                                      ALU.mult).then_inc(job_out["n"].sem, 1)
                    if unit.layer:
                        if i == 0:
                            dve.wait_ge(xres_loaded.sem, xres_loaded.at(unit, DMA))
                        dve.wait_ge(job_out["n"].sem, job_out["n"].at(unit, i + 1))
                        dve.tensor_tensor(x_res[:, i, :], att[:, i, :], x_res[:, i, :],
                                          ALU.add).then_inc(summed.sem, 1)
                        row_stats(unit, i)
                elif kind == "w":
                    if i == 0:
                        dve.wait_ge(bo_added.sem, bo_added.at(unit, 1))
                    dve.tensor_tensor(x_res[:, i, :], ps_job[:, 0:D], x_res[:, i, :], ALU.add)\
                        .then_inc(summed.sem, 1)
                    row_stats(unit, i)

            def layer_norm_mean(unit):
                for c in range(C):
                    if c == 0:
                        dve.wait_ge(stats_out.sem, stats_out.at(unit, C))
                        carry_wait()
                    dve.bn_aggr(mean_var[:, c, :], stats[:, c, :]).then_inc(mean_out.sem, 1)
                dve.wait_ge(mean_out.sem, mean_out.at(unit, C))
                dve.tensor_scalar(var_eps[:], mean_var[:, :, 1], LN_EPS, None, ALU.add).then_inc(var_out.sem, 1)

            def layer_norm(unit):
                dve.wait_ge(rstd_out.sem, rstd_out.at(unit, 1))
                for c in range(C):
                    done = dve.tensor_scalar(x_res[:, c, :], x_res[:, c, :], mean_var[:, c, 0:1], rstd[:, c:c + 1],
                                             ALU.subtract, ALU.mult)
                done.then_inc(normed.sem, 1)

            def unit(own, post, nxt):
                for p in range(PAIRS):
                    todo = job_at(p - 1, own, post, nxt) if p else None
                    if todo is not None:
                        job(*todo)
                    ahead = p + AHEAD
                    if ahead < PAIRS:
                        maxima(own, ahead)
                    elif nxt is not None:
                        maxima(nxt, ahead - PAIRS)
                    if not ON_ACT[p]:
                        turned_copy(own, p)
                    if p % GH == 3 and p > GH:
                        invert(own, p // GH - 1)
                    elif p == 3 and post is not None:
                        invert(post, BLOCKS - 1)
                    if post is not None:
                        last = 7 if post.layer else 14
                        if p == last:
                            layer_norm_mean(post)
                        if p == last + 1:
                            layer_norm(post)
                    if nxt is not None:
                        if p == 18:
                            make_bias(nxt, 0)
                        if p == 22:
                            make_bias(nxt, 1)
                        if nxt.layer != own.layer and p in (6, 8, 10):
                            split_weight(4 + (p - 6) // 2)

            dve.wait_ge(setup_loaded.sem, 6 * DMA)
            dve.tensor_scalar(bq_col[:], bq_col[:], scale[4], None, ALU.mult).then_inc(setup_scaled.sem, 1)
            for i in range(4):
                split_weight(i)
            make_bias(Unit(0, 0), 0)
            make_bias(Unit(0, 0), 1)
            for kind, i in FIRST_JOBS:
                job(kind, Unit(0, 0), i)
            for p in range(AHEAD):
                maxima(Unit(0, 0), p)
            units(dve, unit)
            invert(LAST, BLOCKS - 1)
            for i in range(C):
                job("n", LAST, i)
            layer_norm_mean(LAST)
            layer_norm(LAST)


_INS = ["x", "adj", "L0_gnn_Wq", "L0_gnn_Wk", "L0_gnn_Wv", "L0_gnn_bv", "L0_gnn_Wo", "L0_gnn_bo",
        "L1_gnn_Wq", "L1_gnn_bq", "L1_gnn_Wk", "L1_gnn_bk", "L1_gnn_Wv", "L1_gnn_bv", "L1_gnn_beta"]
_TRANSPOSED = ("L0_gnn_Wq", "L0_gnn_Wk", "L0_gnn_Wv", "L0_gnn_Wo")


def kernel(**inputs):
    import numpy as _np
    import concourse.bacc as _bacc
    from concourse import mybir as _mybir
    from concourse.bass_utils import run_bass_kernel_spmd as _run

    nc = _bacc.Bacc("TRN2", target_bir_lowering=False, num_devices=1)
    arrays, args = {}, []
    for name in _INS:
        a = _np.asarray(inputs[name])
        if name in _TRANSPOSED:
            a = a.T
        a = _np.ascontiguousarray(a.reshape(1) if a.ndim == 0 else a)
        arrays[f"in_{name}_dram"] = a
        args.append(nc.dram_tensor(f"in_{name}_dram", a.shape, _mybir.dt.from_np(a.dtype), kind="ExternalInput").ap())
    o = nc.dram_tensor("out_0_dram", (B, N, D), F32, kind="ExternalOutput").ap()
    two_layer_graph_attention(nc, *args, o)
    r = _run(nc, [arrays], core_ids=[0])
    return r.results[0]["out_0_dram"]
```

```python
from contextlib import ExitStack

import concourse.bass as bass
from concourse import mybir

F32 = mybir.dt.float32
F32R = mybir.dt.float32r
ALU = mybir.AluOpType
ACT = mybir.ActivationFunctionType

P = 128
B, N, D, H = 16, 512, 384, 12
HD = D // H
GH = P // HD
G = H // GH
C = N // P
HALF = N // 2
BLOCKS = 2 * G
PAIRS = GH * BLOCKS
AHEAD = 3
STACK = 3 * HD
RING = 3
MASKED = -9000000000000000.0
LN_EPS = 1e-5
BIG = 3.0e38
DMA = 16

SLOTS = AHEAD + 1
TBANKS = 3

SLOTS_OF_UNIT = 2 * PAIRS
PARTS = {"x": 1, "q": 1, "k": 2, "v": 2, "n": 1, "b": 1, "w": 2}
SCHEDULES = (
    [("n", "post", 0, 6), ("n", "post", 1, 7), ("n", "post", 2, 8), ("b", "post", 0, 9),
     ("b", "post", 1, 10), ("b", "post", 2, 11), ("n", "post", 3, 12), ("q", "own", 2, 14),
     ("k", "own", 2, 15), ("b", "post", 3, 17), ("w", "post", 0, 19), ("w", "post", 1, 20),
     ("w", "post", 2, 22), ("w", "post", 3, 24), ("x", "next", 0, 25), ("x", "next", 1, 26),
     ("x", "next", 2, 27), ("q", "next", 0, 30), ("k", "next", 0, 31), ("v", "next", 0, 35),
     ("v", "next", 1, 36), ("v", "next", 2, 38), ("v", "next", 3, 41), ("q", "next", 1, 41),
     ("k", "next", 1, 45)],
    [("n", "post", 0, 6), ("n", "post", 1, 7), ("n", "post", 2, 9), ("q", "own", 2, 10),
     ("n", "post", 3, 13), ("k", "own", 2, 14), ("x", "next", 0, 20), ("x", "next", 1, 21),
     ("x", "next", 2, 22), ("v", "next", 0, 24), ("q", "next", 0, 27), ("k", "next", 0, 30),
     ("v", "next", 1, 34), ("v", "next", 2, 35), ("v", "next", 3, 38), ("q", "next", 1, 42),
     ("k", "next", 1, 45)],
)
FIRST_JOBS = [("x", 0), ("x", 1), ("x", 2), ("q", 0), ("k", 0), ("v", 0), ("v", 1), ("v", 2), ("v", 3),
              ("q", 1), ("k", 1)]

WEIGHT_SLOTS = (18, 24, 30)
BIAS_SLOTS = (36, 38, 41, 45)
NORM_SLOT = (29, 15)
NORMED_SLOT = (30, 20)


def bank(order, n):
    return (len(order) - n) % 2


ON_DVE = (1, 4, 6, 9, 18, 23, 24, 30, 31, 32, 35, 36, 39, 41, 42, 46)
ON_ACT = [t not in ON_DVE for t in range(SLOTS_OF_UNIT)]


class Unit:

    def __init__(self, layer, graph):
        self.layer, self.graph = layer, graph

    def before(self):
        if self.layer and isinstance(self.graph, int) and self.graph == 0:
            return Unit(0, B - 1)
        return Unit(self.layer, self.graph - 1)


class Signal:

    def __init__(self, sem, layer0, layer1=None):
        self.sem = sem
        self.per = (layer0, layer0 if layer1 is None else layer1)

    def at(self, unit, count):
        return unit.graph * self.per[unit.layer] + (unit.layer * B * self.per[0] + count)

    def begun(self, unit, count):
        value = self.at(unit, count)
        return not isinstance(value, int) or value > 0


def place(p):
    block = p // GH
    return block, block // 2, block % 2, p % GH


def two_layer_graph_attention(nc, x, adj, wq0, wk0, wv0, bv0, wo0, bo0,
                              wq1, bq1, wk1, bk1, wv1, bv1, beta, out):
    with ExitStack() as ctx:
        def sb(name, shape, dt=F32):
            return ctx.enter_context(nc.sbuf_tensor(name, [P] + shape, dt))

        def signal(name, layer0=1, layer1=None):
            return Signal(ctx.enter_context(nc.semaphore(name)), layer0, layer1)

        x1 = nc.dram_tensor("x1_scratch", [B, N, D], F32, kind="Internal").ap()

        ident = sb("ident", [P])
        raw = sb("raw", [G * D])
        adj_raw = raw[:, 0:2 * N].rearrange("p (c n) -> p c n", c=2)
        w_hi = sb("w_hi", [3, G, D], F32R)
        w_lo = sb("w_lo", [3, G, D], F32R)
        wo_hi = sb("wo_hi", [G, D], F32R)
        wo_lo = sb("wo_lo", [G, D], F32R)
        bq_col = sb("bq_col", [G])
        bk_col = sb("bk_col", [G])
        bv_row = sb("bv_row", [2, D])
        bo_row = sb("bo_row", [D])
        beta_col = sb("beta_col", [1])
        pow_col = sb("pow_col", [C])
        bias = sb("bias", [C, N])
        x_in = sb("x_in", [C, D])
        v_new = x_in
        att = x_in
        x_res = sb("x_res", [C, D])
        xT_hi = sb("xT_hi", [G, N], F32R)
        xT_lo = sb("xT_lo", [G, N], F32R)
        attT_hi = sb("attT_hi", [G, N], F32R)
        attT_lo = sb("attT_lo", [G, N], F32R)
        qk = sb("qk", [4, N], F32R)
        q_lo, q_hi, k_hi, k_lo = (qk[:, i, :] for i in range(4))
        stack = sb("stack", [H, 2, N], F32R)
        v_sb = sb("v_sb", [G, C, P])
        minus_s = sb("minus_s", [SLOTS, 2, N])
        probs = minus_s
        row_tmp = sb("row_tmp", [D])
        probsT = sb("probsT", [2, GH, C, HALF])
        minus_max = sb("minus_max", [RING, 2, GH])
        sums = sb("sums", [RING, 2, GH])
        zero_row = sb("zero_row", [2, GH])
        rinv = sb("rinv", [C, H])
        oT = sb("oT", [G, N])
        stats = sb("stats", [C, 6])
        mean_var = sb("mean_var", [C, 2])
        var_eps = sb("var_eps", [C])
        rstd = sb("rstd", [C])

        ps_s = ctx.enter_context(nc.psum_tensor("ps_s", [P, 2, N], F32))
        ps_t = ctx.enter_context(nc.psum_tensor("ps_t", [P, TBANKS, C, P], F32))
        ps_o = ctx.enter_context(nc.psum_tensor("ps_o", [P, N], F32))
        ps_jobs = ctx.enter_context(nc.psum_tensor("ps_jobs", [P, 2, N], F32))

        setup_loaded = signal("setup_loaded")
        setup_pool = signal("setup_pool")
        setup_scaled = signal("setup_scaled")
        w_loaded = [signal(f"w_loaded{i}") for i in range(7)]
        w_hi_out, w_lo_out = signal("w_hi_out"), signal("w_lo_out")
        raw_loaded = signal("raw_loaded", 2 * DMA)
        xin_loaded = signal("xin_loaded", DMA)
        xres_loaded = signal("xres_loaded", DMA)
        stored = signal("stored", DMA)
        stacked = [signal(f"stacked{h}", 3 * DMA) for h in range(H)]
        scored = signal("scored", 2 * PAIRS)
        maxed = signal("maxed", 2 * PAIRS)
        expd = signal("expd", 2 * PAIRS)
        turned = signal("turned", 2 * PAIRS)
        turned_out_act = signal("turned_out_act", sum(ON_ACT))
        turned_out_dve = signal("turned_out_dve", 2 * PAIRS - sum(ON_ACT))
        o_ready, o_out = signal("o_ready", BLOCKS), signal("o_out", BLOCKS)
        per_job = {"x": (G, G), "q": (G, G), "k": (G, G), "v": (C, C), "n": (C, C), "b": (C, 0), "w": (C, 0)}
        job_ready = {j: signal(f"{j}_ready", *n) for j, n in per_job.items()}
        job_hi = {j: signal(f"{j}_hi_out", *per_job[j]) for j in "xqkb"}
        summed = signal("summed", C)
        job_out = {j: signal(f"{j}_out", *per_job[j]) for j in "xqkvnb"} | {"w": summed}
        inverted = signal("inverted", BLOCKS)
        inverting = signal("inverting", 4 * BLOCKS, BLOCKS)
        bias_masked = signal("bias_masked", 0, C)
        bias_out = signal("bias_out", C)
        stats_out = signal("stats_out", C)
        mean_out = signal("mean_out", C)
        var_out = signal("var_out", 1)
        rstd_out = signal("rstd_out", 1)
        normed = signal("normed", 1)
        v_placed = signal("v_placed", G)
        bo_added = signal("bo_added", 1, 0)
        waits_carried = signal("waits_carried")

        def nodes(t, unit):
            return t[unit.graph].rearrange("(c p) d -> p c d", p=P)

        def turned_out(t):
            act = sum(ON_ACT[:t % (2 * PAIRS) + 1]) + t // (2 * PAIRS) * sum(ON_ACT)
            return (turned_out_act, act) if ON_ACT[t] else (turned_out_dve, t + 1 - act)

        def jobs_in(slot, own, post, nxt):
            jobs = SCHEDULES[0 if post is None else post.layer]
            found = []
            for n, (kind, whose, i, start) in enumerate(jobs):
                unit = {"own": own, "post": post, "next": nxt}[whose]
                if unit is not None and start <= slot < start + PARTS[kind]:
                    found.append((kind, unit, i, slot - start, bank(jobs, n)))
            return found

        def jobs_done(slot, own, post, nxt):
            return [(kind, unit, i, b) for kind, unit, i, part, b in jobs_in(slot, own, post, nxt)
                    if part == PARTS[kind] - 1]

        def first_jobs():
            return [(kind, Unit(0, 0), i, bank(FIRST_JOBS, n)) for n, (kind, i) in enumerate(FIRST_JOBS)]

        def last_jobs():
            return [("n", LAST, i, i % 2) for i in range(C)]

        def coming(slot, own, nxt):
            unit, t = (own, slot + 2 * AHEAD) if slot + 2 * AHEAD < SLOTS_OF_UNIT \
                else (nxt, slot + 2 * AHEAD - SLOTS_OF_UNIT)
            return None if unit is None else (unit, t // 2, t % 2)

        def units(eng, body):
            body(Unit(0, 0), None, Unit(0, 1))
            with eng.Fori(1, B - 1) as graph:
                body(Unit(0, graph), Unit(0, graph - 1), Unit(0, graph + 1))
            body(Unit(0, B - 1), Unit(0, B - 2), Unit(1, 0))
            body(Unit(1, 0), Unit(0, B - 1), Unit(1, 1))
            with eng.Fori(1, B - 1) as graph:
                body(Unit(1, graph), Unit(1, graph - 1), Unit(1, graph + 1))
            body(Unit(1, B - 1), Unit(1, B - 2), None)

        LAST = Unit(1, B - 1)
        def w_raw(i):
            at = probsT[:].rearrange("p b h c q -> p (b h c q)")[:, G * D * i:G * D * i + G * D] if i < 4 else raw[:]
            return at.rearrange("p (t n) -> p t n", t=G)

        weights = [(wq0, 0), (wk0, 1), (wv0, 2), (wo0, None), (wq1, 0), (wk1, 1), (wv1, 2)]
        scale = {0: float(D) ** -0.5, 4: float(HD) ** -0.5}

        block = ctx.enter_context(nc.Block())

        @block.sync
        def _(sp):
            def load_weight(i):
                if i > 4:
                    sp.wait_ge(w_lo_out.sem, i)
                sp.dma_start(w_raw(i), weights[i][0].rearrange("(t p) n -> p t n", p=P)).then_inc(w_loaded[i].sem, DMA)

            def load_adj(unit, half):
                if bias_out.begun(unit, 2 * half):
                    sp.wait_ge(bias_out.sem, bias_out.at(unit, 2 * half))
                sp.dma_start(adj_raw, nodes(adj, unit)[:, 2 * half:2 * half + 2, :]).then_inc(raw_loaded.sem, DMA)

            def load_xin(unit, own, post):
                source = x1 if unit.layer else x
                if own is not None:
                    sp.wait_ge(v_placed.sem, v_placed.at(own, G))
                if post is not None and post.layer == 0:
                    sp.wait_ge(job_ready["b"].sem, job_ready["b"].at(post, C))
                sp.dma_start(x_in[:], nodes(source, unit)).then_inc(xin_loaded.sem, DMA)

            def load_xres(unit):
                sp.dma_start(x_res[:], nodes(x1 if unit.layer else x, unit)).then_inc(xres_loaded.sem, DMA)

            def store(post):
                sp.wait_ge(normed.sem, normed.at(post, 1))
                target = out if post.layer else x1
                sp.dma_start(nodes(target, post), x_res[:]).then_inc(stored.sem, DMA)
                sp.wait_ge(stored.sem, stored.at(post, DMA))

            def stack_group(unit, g):
                sp.wait_ge(job_out["q"].sem, job_out["q"].at(unit, g + 1))
                sp.wait_ge(job_out["k"].sem, job_out["k"].at(unit, g + 1))
                for h in range(GH):
                    for row, (first, step) in enumerate(((1, 1), (0, 2), (1, 2))):
                        sp.dma_start(stack[HD * row:HD * row + HD, GH * g + h].bitcast(F32),
                                     qk[HD * h:HD * h + HD, first:first + step + 1:step, :].bitcast(F32))\
                            .then_inc(stacked[GH * g + h].sem, DMA)

            def unit(own, post, nxt):
                stack_group(own, 1)
                if nxt is not None:
                    if nxt.layer == own.layer:
                        load_adj(nxt, 0)
                    else:
                        sp.wait_ge(bias_out.sem, bias_out.at(own, C))
                        load_weight(4)
                    load_xin(nxt, own, post)
                stack_group(own, 2)
                if nxt is not None and nxt.layer != own.layer:
                    load_weight(5)
                    load_weight(6)
                if post is not None:
                    store(post)
                    load_xres(own)
                if nxt is not None:
                    if nxt.layer != own.layer:
                        sp.wait_ge(w_lo_out.sem, 7)
                        load_adj(nxt, 0)
                    stack_group(nxt, 0)
                    load_adj(nxt, 1)

            first = Unit(0, 0)
            load_xin(first, None, None)
            for i in range(3):
                load_weight(i)
            load_adj(first, 0)
            sp.dma_start(bv_row[:, 0, :], bv0.partition_broadcast(P)).then_inc(setup_loaded.sem, DMA)
            sp.dma_start(bv_row[:, 1, :], bv1.partition_broadcast(P)).then_inc(setup_loaded.sem, DMA)
            sp.dma_start(bo_row[:], bo0.partition_broadcast(P)).then_inc(setup_loaded.sem, DMA)
            sp.dma_start(beta_col[:], beta.partition_broadcast(P)).then_inc(setup_loaded.sem, DMA)
            sp.dma_start(bq_col[:], bq1.rearrange("(g p) -> p g", p=P),
                         allow_slow_non_contiguous=True).then_inc(setup_loaded.sem, DMA)
            sp.dma_start(bk_col[:], bk1.rearrange("(g p) -> p g", p=P),
                         allow_slow_non_contiguous=True).then_inc(setup_loaded.sem, DMA)
            stack_group(first, 0)
            load_weight(3)
            load_xres(first)
            load_adj(first, 1)
            units(sp, unit)
            store(LAST)

        @block.gpsimd
        def _(pool):
            pool.memset(ident[:], 0.0).then_inc(setup_pool.sem, 1)
            pool.memset(pow_col[:], -0.5).then_inc(setup_pool.sem, 1)
            pool.wait_ge(setup_pool.sem, 2)
            pool.affine_select(out=ident[:], in_=ident[:], compare_op=ALU.not_equal, fill=1.0, base=0,
                               pattern=[[-1, P]], channel_multiplier=1).then_inc(setup_pool.sem, 1)

            def post_stage(post):
                if post.layer == 0:
                    pool.wait_ge(xres_loaded.sem, xres_loaded.at(post, DMA))
                    pool.tensor_tensor(x_res[:], x_res[:], bo_row[:, None, :].to_broadcast([P, C, D]),
                                       ALU.add).then_inc(bo_added.sem, 1)
                else:
                    pool.wait_ge(xres_loaded.sem, xres_loaded.at(post, DMA))
                    for c in range(C):
                        pool.wait_ge(job_out["n"].sem, job_out["n"].at(post, c + 1))
                        pool.tensor_tensor(x_res[:, c, :], row_tmp[:], x_res[:, c, :],
                                           ALU.add).then_inc(summed.sem, 1)
                pool.wait_ge(var_out.sem, var_out.at(post, 1))
                pool.tensor_tensor(rstd[:], var_eps[:], pow_col[:], ALU.pow).then_inc(rstd_out.sem, 1)

            def place_values(unit, g):
                pool.wait_ge(job_out["v"].sem, job_out["v"].at(unit, C))
                before = unit.before()
                if o_ready.begun(before, 2 * g + 2):
                    pool.wait_ge(o_ready.sem, o_ready.at(before, 2 * g + 2))
                cols = slice(P * g, P * g + P)
                pool.tensor_tensor(v_sb[:, g], v_new[:, :, cols],
                                   bv_row[:, unit.layer, None, cols].to_broadcast([P, C, P]),
                                   ALU.add).then_inc(v_placed.sem, 1)

            def unit(own, post, nxt):
                place_values(own, 2)
                if post is not None:
                    post_stage(post)
                if nxt is not None:
                    place_values(nxt, 0)
                    place_values(nxt, 1)

            pool.wait_ge(setup_loaded.sem, 6 * DMA)
            place_values(Unit(0, 0), 0)
            place_values(Unit(0, 0), 1)
            units(pool, unit)
            post_stage(LAST)

        @block.tensor
        def _(pe):
            def products(ps, a, b, part, of):
                terms = [(s, m, t) for s, m in ((a[0], b[0]), (a[0], b[1]), (a[1], b[0])) for t in range(G)]
                size = -(-len(terms) // of)
                for k, (s, m, t) in enumerate(terms):
                    if k // size == part:
                        mm = pe.matmul(ps, s(t), m(t), start=(k == 0), stop=(k == len(terms) - 1))
                return mm

            def cols(tile, *at):
                lead, (a, b) = at[:-1], at[-1]
                return lambda t: tile[(slice(None), *lead, t, slice(a, b))]

            def job(kind, unit, i, part, ps_job):
                of = PARTS[kind]
                w = w_hi, w_lo
                xT = xT_hi, xT_lo
                if kind == "x":
                    if i == 0:
                        pe.wait_ge(xin_loaded.sem, xin_loaded.at(unit, DMA))
                    for c in range(C):
                        mm = pe.transpose(ps_job[:, P * c:P * c + P], x_in[:, c, P * i:P * i + P], ident[:])
                elif kind in "qk":
                    m = "qk".index(kind)
                    pe.wait_ge(job_out["x"].sem, job_out["x"].at(unit, G))
                    pe.wait_ge(w_lo_out.sem, 4 * unit.layer + m + 1)
                    mm = products(ps_job, [cols(t, m, (P * i, P * i + P)) for t in w],
                                  [cols(t, (0, N)) for t in xT], part, of)
                elif kind == "v":
                    if i == 0 and part == 0:
                        pe.wait_ge(job_out["x"].sem, job_out["x"].at(unit, G))
                        pe.wait_ge(w_lo_out.sem, 4 * unit.layer + 3)
                    mm = products(ps_job[:, 0:D], [cols(t, (P * i, P * i + P)) for t in xT],
                                  [cols(t, 2, (0, D)) for t in w], part, of)
                elif kind == "n":
                    if i == 0:
                        pe.wait_ge(o_out.sem, o_out.at(unit, BLOCKS))
                    for g in range(G):
                        mm = pe.transpose(ps_job[:, P * g:P * g + P], oT[:, g, P * i:P * i + P], ident[:])
                elif kind == "b":
                    pe.wait_ge(job_out["n"].sem, job_out["n"].at(unit, i + 1))
                    for g in range(G):
                        mm = pe.transpose(ps_job[:, P * g:P * g + P], att[:, i, P * g:P * g + P], ident[:])
                elif kind == "w":
                    if i == 0:
                        pe.wait_ge(w_lo_out.sem, 4)
                    pe.wait_ge(job_out["b"].sem, job_out["b"].at(unit, i + 1))
                    mm = products(ps_job[:, 0:D], [cols(t, (P * i, P * i + P)) for t in (attT_hi, attT_lo)],
                                  [cols(t, (0, D)) for t in (wo_hi, wo_lo)], part, of)
                if part == of - 1:
                    mm.then_inc(job_ready[kind].sem, 1)

            holder = {}

            def side_job(kind, unit, i, part, bank):
                if part == 0:
                    if bank in holder:
                        before, its_unit, n = holder[bank]
                        pe.wait_ge(job_out[before].sem, job_out[before].at(its_unit, n + 1))
                    holder[bank] = kind, unit, i
                job(kind, unit, i, part, ps_jobs[:, bank])

            def score(unit, p, c):
                _, g, half, h = place(p)
                head = GH * g + h
                if half == 0 and c == 0:
                    pe.wait_ge(stacked[head].sem, stacked[head].at(unit, 3 * DMA))
                if maxed.begun(unit, 2 * p + c - 1):
                    pe.wait_ge(maxed.sem, maxed.at(unit, 2 * p + c - 1))
                q0 = P * (2 * half + c)
                pe.matmul(ps_s[:, c, :], stack[0:STACK, head, 0, q0:q0 + P],
                          stack[0:STACK, head, 1, :], start=True, stop=True).then_inc(scored.sem, 1)

            def turn(unit, p, c):
                t = 2 * p + c
                out_of_bank, count = turned_out(t - TBANKS)
                if out_of_bank.begun(unit, count):
                    pe.wait_ge(out_of_bank.sem, out_of_bank.at(unit, count))
                pe.wait_ge(expd.sem, expd.at(unit, t + 1))
                for kc in range(C):
                    mm = pe.transpose(ps_t[:, t % TBANKS, kc, :], probs[:, p % SLOTS, c, P * kc:P * kc + P], ident[:])
                mm.then_inc(turned.sem, 1)

            def weigh_values(unit, b, kc):
                g, half = b // 2, b % 2
                if half == 0 and kc == 0:
                    pe.wait_ge(v_placed.sem, v_placed.at(unit, g + 1))
                if kc == 0:
                    end = 2 * GH * (b + 1)
                    for t in {ON_ACT[t]: t for t in range(end - 8, end)}.values():
                        in_sbuf, count = turned_out(t)
                        pe.wait_ge(in_sbuf.sem, in_sbuf.at(unit, count))
                    if o_out.begun(unit, b):
                        pe.wait_ge(o_out.sem, o_out.at(unit, b))
                for h in range(GH):
                    mm = pe.matmul(ps_o[HD * h:HD * h + HD, HALF * half:HALF * half + HALF],
                                   v_sb[:, g, kc, HD * h:HD * h + HD], probsT[:, b % 2, h, kc, :],
                                   start=(kc == 0), stop=(kc == C - 1))
                if kc == C - 1:
                    mm.then_inc(o_ready.sem, 1)

            def unit(own, post, nxt):
                holder.update({0: ("q", own, 1), 1: ("k", own, 1)})
                for slot in range(SLOTS_OF_UNIT):
                    scoring = coming(slot, own, nxt)
                    if scoring is not None:
                        score(*scoring)
                    turn(own, slot // 2, slot % 2)
                    kc = slot % (2 * GH) - 1
                    if 0 <= kc < C:
                        if slot > 2 * GH:
                            weigh_values(own, slot // (2 * GH) - 1, kc)
                        elif post is not None:
                            weigh_values(post, BLOCKS - 1, kc)
                    for todo in jobs_in(slot, own, post, nxt):
                        side_job(*todo)

            pe.wait_ge(setup_pool.sem, 3)
            for kind, its_unit, i, b in first_jobs():
                for part in range(PARTS[kind]):
                    side_job(kind, its_unit, i, part, b)
            for t in range(2 * AHEAD):
                score(Unit(0, 0), t // 2, t % 2)
            units(pe, unit)
            for kc in range(C):
                weigh_values(LAST, BLOCKS - 1, kc)
            holder.clear()
            for kind, its_unit, i, b in last_jobs():
                side_job(kind, its_unit, i, 0, b)

        @block.scalar
        def _(act):
            def split_weight(i):
                m = weights[i][1]
                act.wait_ge(w_loaded[i].sem, DMA)
                if i == 4:
                    act.wait_ge(job_ready["k"].sem, job_ready["k"].at(Unit(0, B - 1), G))
                hi = wo_hi[:] if m is None else w_hi[:, m]
                act.activation(hi, w_raw(i), ACT.Copy, scale=scale.get(i, 1.0)).then_inc(w_hi_out.sem, 1)

            def job(kind, unit, i, bank):
                if kind not in "xqkbv":
                    return
                ps_job = ps_jobs[:, bank]
                act.wait_ge(job_ready[kind].sem, job_ready[kind].at(unit, i + 1))
                if kind == "v":
                    if v_placed.begun(unit, 0):
                        act.wait_ge(v_placed.sem, v_placed.at(unit, 0))
                    act.activation(v_new[:, i, :], ps_job[:, 0:D], ACT.Copy).then_inc(job_out["v"].sem, 1)
                    return
                if kind == "b":
                    act.activation(attT_hi[:, :, P * i:P * i + P], ps_job[:, 0:D].rearrange("p (g q) -> p g q", g=G),
                                   ACT.Copy).then_inc(job_hi["b"].sem, 1)
                    return
                if kind in "qk":
                    before, g = (unit, i - 1) if i else (unit.before(), G - 1)
                    for head in range(GH * g, GH * g + GH):
                        if stacked[head].begun(before, 3 * DMA):
                            act.wait_ge(stacked[head].sem, stacked[head].at(before, 3 * DMA))
                to = {"x": xT_hi[:, i, :], "q": q_hi, "k": k_hi}[kind]
                if kind in "qk" and unit.layer:
                    col = (bq_col if kind == "q" else bk_col)[:, i:i + 1]
                    done = act.activation(to, ps_job, ACT.Identity, bias=col)
                else:
                    done = act.activation(to, ps_job, ACT.Copy)
                done.then_inc(job_hi[kind].sem, 1)

            def exponentials(unit, p, c):
                b, _, _, h = place(p)
                if p % GH == 0 and c == 0:
                    if inverted.begun(unit, b - RING + 1):
                        act.wait_ge(inverted.sem, inverted.at(unit, b - RING + 1))
                act.wait_ge(maxed.sem, maxed.at(unit, 2 * p + c + 1))
                act.activation(probs[:, p % SLOTS, c, :], minus_s[:, p % SLOTS, c, :], ACT.Exp,
                               bias=minus_max[:, b % RING, c, h:h + 1], scale=-1.0,
                               accum_out=sums[:, b % RING, c, h:h + 1]).then_inc(expd.sem, 1)

            def turned_copy(unit, t):
                b, _, _, h = place(t // 2)
                c = t % 2
                if o_ready.begun(unit, b - 1):
                    act.wait_ge(o_ready.sem, o_ready.at(unit, b - 1))
                act.wait_ge(turned.sem, turned.at(unit, t + 1))
                act.activation(probsT[:, b % 2, h, :, P * c:P * c + P], ps_t[:, t % TBANKS],
                               ACT.Copy).then_inc(turned_out_act.sem, 1)

            def o_copy(unit, b):
                g, half = b // 2, b % 2
                act.wait_ge(o_ready.sem, o_ready.at(unit, b + 1))
                if g == 0:
                    if job_ready["n"].begun(unit.before(), 2 * half + 2):
                        act.wait_ge(job_ready["n"].sem, job_ready["n"].at(unit.before(), 2 * half + 2))
                cols = slice(HALF * half, HALF * half + HALF)
                act.activation(oT[:, g, cols], ps_o[:, cols], ACT.Copy).then_inc(o_out.sem, 1)

            def unit(own, post, nxt):
                for slot in range(SLOTS_OF_UNIT):
                    if slot:
                        for todo in jobs_done(slot - 1, own, post, nxt):
                            job(*todo)
                    if slot % (2 * GH) == C + 1:
                        if slot > 2 * GH:
                            o_copy(own, slot // (2 * GH) - 1)
                        elif post is not None:
                            o_copy(post, BLOCKS - 1)
                    if ON_ACT[slot]:
                        turned_copy(own, slot)
                    scoring = coming(slot, own, nxt)
                    if scoring is not None:
                        exponentials(*scoring)
                    if nxt is not None and nxt.layer != own.layer and slot in WEIGHT_SLOTS:
                        split_weight(4 + WEIGHT_SLOTS.index(slot))

            for todo in first_jobs()[:G]:
                job(*todo)
            for i in range(3):
                split_weight(i)
            for todo in first_jobs()[G:]:
                job(*todo)
            split_weight(3)
            act.wait_ge(setup_scaled.sem, 1)
            for t in range(2 * AHEAD):
                exponentials(Unit(0, 0), t // 2, t % 2)
            units(act, unit)
            o_copy(LAST, BLOCKS - 1)

        @block.vector
        def _(dve):
            def carry_wait():
                dve.sem_inc(waits_carried.sem, 1)

            def split_weight(i):
                m = weights[i][1]
                dve.wait_ge(w_hi_out.sem, i + 1)
                hi, lo = (wo_hi[:], wo_lo[:]) if m is None else (w_hi[:, m], w_lo[:, m])
                flat = "p t n -> p (t n)"
                dve.scalar_tensor_tensor(lo.rearrange(flat), w_raw(i).rearrange(flat), scale.get(i, 1.0),
                                         hi.bitcast(F32).rearrange(flat), ALU.mult,
                                         ALU.subtract).then_inc(w_lo_out.sem, 1)

            def make_bias(unit, c):
                raw_rows, to = adj_raw[:, c % 2, :], bias[:, c, :]
                before, last = unit.before(), 2 * GH * (BLOCKS - 1 + c // 2) - 1 + c % 2
                if maxed.begun(before, last):
                    dve.wait_ge(maxed.sem, maxed.at(before, last))
                if c % 2 == 0:
                    dve.wait_ge(raw_loaded.sem, raw_loaded.at(unit, DMA * (c // 2 + 1)))
                if unit.layer == 0:
                    dve.tensor_scalar(to, raw_rows, 2.0, None, ALU.mult).then_inc(bias_out.sem, 1)
                else:
                    dve.tensor_scalar(to, raw_rows, 0.0, MASKED, ALU.is_le, ALU.mult).then_inc(bias_masked.sem, 1)
                    dve.wait_ge(bias_masked.sem, bias_masked.at(unit, c + 1))
                    dve.scalar_tensor_tensor(to, raw_rows, beta_col[:, 0:1], to, ALU.mult,
                                             ALU.add).then_inc(bias_out.sem, 1)

            def maxima(unit, p, c):
                b, g, half, h = place(p)
                if h == 0 and g == 0:
                    dve.wait_ge(bias_out.sem, bias_out.at(unit, 2 * half + c + 1))
                dve.wait_ge(scored.sem, scored.at(unit, 2 * p + c + 1))
                carry_wait()
                dve.tensor_tensor_reduce(minus_s[:, p % SLOTS, c, :], ps_s[:, c, :], bias[:, 2 * half + c, :],
                                         -1.0, BIG, ALU.add, ALU.min,
                                         minus_max[:, b % RING, c, h:h + 1]).then_inc(maxed.sem, 1)

            def invert(unit, b):
                g, half = b // 2, b % 2
                to = rinv[:, 2 * half:2 * half + 2, GH * g:GH * g + GH]
                dve.wait_ge(expd.sem, expd.at(unit, 2 * GH * (b + 1)))
                s, m = sums[:, b % RING], minus_max[:, b % RING]
                if unit.layer:
                    dve.reciprocal(to, s).then_inc(inverted.sem, 1)
                    return
                dve.reciprocal(to, s).then_inc(inverting.sem, 1)
                dve.tensor_scalar(zero_row[:], s, float(N), None, ALU.is_equal).then_inc(inverting.sem, 1)
                dve.wait_ge(inverting.sem, inverting.at(unit, 4 * b + 2))
                dve.scalar_tensor_tensor(zero_row[:], m, 0.0, zero_row[:], ALU.is_equal,
                                         ALU.mult).then_inc(inverting.sem, 1)
                dve.wait_ge(inverting.sem, inverting.at(unit, 4 * b + 3))
                dve.tensor_scalar(zero_row[:], zero_row[:], -1.0, 1.0, ALU.mult, ALU.add).then_inc(inverting.sem, 1)
                dve.wait_ge(inverting.sem, inverting.at(unit, 4 * b + 4))
                dve.tensor_tensor(to, to, zero_row[:], ALU.mult).then_inc(inverted.sem, 1)

            def turned_copy(unit, t):
                b, _, _, h = place(t // 2)
                c = t % 2
                if o_ready.begun(unit, b - 1):
                    dve.wait_ge(o_ready.sem, o_ready.at(unit, b - 1))
                dve.wait_ge(turned.sem, turned.at(unit, t + 1))
                dve.tensor_copy(probsT[:, b % 2, h, :, P * c:P * c + P],
                                ps_t[:, t % TBANKS]).then_inc(turned_out_dve.sem, 1)

            def row_stats(unit, c):
                dve.wait_ge(summed.sem, summed.at(unit, c + 1))
                dve.bn_stats(stats[:, c, :], x_res[:, c, :]).then_inc(stats_out.sem, 1)

            def job(kind, unit, i, bank):
                if kind == "v":
                    return
                ps_job = ps_jobs[:, bank]
                if kind in job_hi:
                    dve.wait_ge(job_hi[kind].sem, job_hi[kind].at(unit, i + 1))
                    if kind == "x":
                        hi, lo = xT_hi[:, i, :], xT_lo[:, i, :]
                    elif kind == "b":
                        hi, lo = attT_hi[:, :, P * i:P * i + P], attT_lo[:, :, P * i:P * i + P]
                    else:
                        hi, lo = (q_hi, q_lo) if kind == "q" else (k_hi, k_lo)
                    if kind == "b":
                        done = dve.tensor_tensor(lo, ps_job[:, 0:D].rearrange("p (g q) -> p g q", g=G),
                                                 hi.bitcast(F32), ALU.subtract)
                    elif kind in "qk" and unit.layer:
                        col = (bq_col if kind == "q" else bk_col)[:, i:i + 1]
                        done = dve.scalar_tensor_tensor(lo, ps_job, col, hi.bitcast(F32), ALU.add, ALU.subtract)
                    else:
                        done = dve.tensor_tensor(lo, ps_job, hi.bitcast(F32), ALU.subtract)
                    done.then_inc(job_out[kind].sem, 1)
                    return
                dve.wait_ge(job_ready[kind].sem, job_ready[kind].at(unit, i + 1))
                if kind == "n":
                    if i == 0 and unit.layer == 0:
                        dve.wait_ge(v_placed.sem, v_placed.at(unit, 2 * G))
                    if i == 0:
                        dve.wait_ge(inverted.sem, inverted.at(unit, BLOCKS))
                    to = row_tmp[:] if unit.layer else att[:, i, :]
                    if unit.layer:
                        dve.wait_ge(summed.sem, summed.at(unit, i))
                    dve.tensor_tensor(to.rearrange("p (h d) -> p h d", h=H),
                                      ps_job[:, 0:D].rearrange("p (h d) -> p h d", h=H),
                                      rinv[:, i, :, None].to_broadcast([P, H, HD]),
                                      ALU.mult).then_inc(job_out["n"].sem, 1)
                    if unit.layer and i:
                        row_stats(unit, i - 1)
                elif kind == "w":
                    if i == 0:
                        dve.wait_ge(bo_added.sem, bo_added.at(unit, 1))
                    dve.tensor_tensor(x_res[:, i, :], ps_job[:, 0:D], x_res[:, i, :], ALU.add)\
                        .then_inc(summed.sem, 1)
                    row_stats(unit, i)

            def layer_norm_mean(unit):
                if unit.layer:
                    row_stats(unit, C - 1)
                for c in range(C):
                    if c == 0:
                        dve.wait_ge(stats_out.sem, stats_out.at(unit, C))
                        carry_wait()
                    dve.bn_aggr(mean_var[:, c, :], stats[:, c, :]).then_inc(mean_out.sem, 1)
                dve.wait_ge(mean_out.sem, mean_out.at(unit, C))
                dve.tensor_scalar(var_eps[:], mean_var[:, :, 1], LN_EPS, None, ALU.add).then_inc(var_out.sem, 1)

            def layer_norm(unit):
                dve.wait_ge(rstd_out.sem, rstd_out.at(unit, 1))
                for c in range(C):
                    done = dve.tensor_scalar(x_res[:, c, :], x_res[:, c, :], mean_var[:, c, 0:1], rstd[:, c:c + 1],
                                             ALU.subtract, ALU.mult)
                done.then_inc(normed.sem, 1)

            def unit(own, post, nxt):
                for slot in range(SLOTS_OF_UNIT):
                    if slot % (2 * GH) == C:
                        if slot > 2 * GH:
                            invert(own, slot // (2 * GH) - 1)
                        elif post is not None:
                            invert(post, BLOCKS - 1)
                    scoring = coming(slot, own, nxt)
                    if scoring is not None:
                        maxima(*scoring)
                    if not ON_ACT[slot]:
                        turned_copy(own, slot)
                    if slot:
                        for todo in jobs_done(slot - 1, own, post, nxt):
                            job(*todo)
                    if post is not None:
                        if slot == NORM_SLOT[post.layer]:
                            layer_norm_mean(post)
                        if slot == NORMED_SLOT[post.layer]:
                            layer_norm(post)
                    if nxt is not None:
                        if slot in BIAS_SLOTS:
                            make_bias(nxt, BIAS_SLOTS.index(slot))
                        if nxt.layer != own.layer and slot in WEIGHT_SLOTS:
                            split_weight(4 + WEIGHT_SLOTS.index(slot))

            for todo in first_jobs()[:G]:
                job(*todo)
            for i in range(3):
                split_weight(i)
            for todo in first_jobs()[G:-2]:
                job(*todo)
            for c in range(2):
                make_bias(Unit(0, 0), c)
            for todo in first_jobs()[-2:]:
                job(*todo)
            for c in range(2, C):
                make_bias(Unit(0, 0), c)
            split_weight(3)
            dve.wait_ge(setup_loaded.sem, 6 * DMA)
            dve.tensor_scalar(bq_col[:], bq_col[:], scale[4], None, ALU.mult).then_inc(setup_scaled.sem, 1)
            for t in range(2 * AHEAD):
                maxima(Unit(0, 0), t // 2, t % 2)
            units(dve, unit)
            invert(LAST, BLOCKS - 1)
            for todo in last_jobs():
                job(*todo)
            layer_norm_mean(LAST)
            layer_norm(LAST)


_INS = ["x", "adj", "L0_gnn_Wq", "L0_gnn_Wk", "L0_gnn_Wv", "L0_gnn_bv", "L0_gnn_Wo", "L0_gnn_bo",
        "L1_gnn_Wq", "L1_gnn_bq", "L1_gnn_Wk", "L1_gnn_bk", "L1_gnn_Wv", "L1_gnn_bv", "L1_gnn_beta"]
_TRANSPOSED = ("L0_gnn_Wq", "L0_gnn_Wk", "L0_gnn_Wv", "L0_gnn_Wo")


def kernel(**inputs):
    import numpy as _np
    import concourse.bacc as _bacc
    from concourse import mybir as _mybir
    from concourse.bass_utils import run_bass_kernel_spmd as _run

    nc = _bacc.Bacc("TRN2", target_bir_lowering=False, num_devices=1)
    arrays, args = {}, []
    for name in _INS:
        a = _np.asarray(inputs[name])
        if name in _TRANSPOSED:
            a = a.T
        a = _np.ascontiguousarray(a.reshape(1) if a.ndim == 0 else a)
        arrays[f"in_{name}_dram"] = a
        args.append(nc.dram_tensor(f"in_{name}_dram", a.shape, _mybir.dt.from_np(a.dtype), kind="ExternalInput").ap())
    o = nc.dram_tensor("out_0_dram", (B, N, D), F32, kind="ExternalOutput").ap()
    two_layer_graph_attention(nc, *args, o)
    r = _run(nc, [arrays], core_ids=[0])
    return r.results[0]["out_0_dram"]
```

```python
from contextlib import ExitStack

import concourse.bass as bass
from concourse import mybir

F32 = mybir.dt.float32
F32R = mybir.dt.float32r
ALU = mybir.AluOpType
ACT = mybir.ActivationFunctionType

P = 128
B, N, D, H = 16, 512, 384, 12
HD = D // H
GH = P // HD
G = H // GH
C = N // P
HALF = N // 2
BLOCKS = 2 * G
PAIRS = GH * BLOCKS
AHEAD = 3
STACK = 3 * HD
RING = 3
MASKED = -9000000000000000.0
LN_EPS = 1e-5
BIG = 3.0e38
DMA = 16

HELD = AHEAD + 1
TBANKS = 3

SLOTS_OF_UNIT = 2 * PAIRS
PARTS = {"x": 1, "q": 1, "k": 2, "v": 2, "n": 1, "w": 1, "r": 1}
SCHEDULES = (
    [("r", "post", 0, 8), ("r", "post", 1, 9), ("r", "post", 2, 10), ("q", "own", 2, 12),
     ("k", "own", 2, 15), ("w", "post", 0, 20), ("w", "post", 1, 22), ("w", "post", 2, 23),
     ("w", "post", 3, 24), ("x", "next", 0, 25), ("x", "next", 1, 26), ("x", "next", 2, 27),
     ("q", "next", 0, 30), ("k", "next", 0, 31), ("v", "next", 0, 33), ("v", "next", 1, 35),
     ("v", "next", 2, 37), ("v", "next", 3, 39), ("q", "next", 1, 42), ("k", "next", 1, 45)],
    [("n", "post", 0, 8), ("n", "post", 1, 9), ("n", "post", 2, 10), ("n", "post", 3, 11),
     ("q", "own", 2, 13), ("k", "own", 2, 15), ("x", "next", 0, 17), ("x", "next", 1, 24),
     ("x", "next", 2, 25), ("q", "next", 0, 29), ("k", "next", 0, 30), ("v", "next", 0, 32),
     ("v", "next", 1, 36), ("v", "next", 2, 39), ("v", "next", 3, 40), ("q", "next", 1, 41),
     ("k", "next", 1, 45)],
)
FIRST_JOBS = [("x", 0), ("x", 1), ("x", 2), ("q", 0), ("k", 0), ("v", 0), ("v", 1), ("v", 2), ("v", 3),
              ("q", 1), ("k", 1)]

WEIGHT_SLOTS = (18, 24, 30)
BIAS_SLOTS = (36, 38, 41, 45)
NORM_SLOT = (26, 13)
NORMED_SLOT = (30, 27)
WEIGH_AT = {1: (0,), 3: (1, 2), 4: (3,)}
O_COPY_AT = 5
ON_DVE = (3, 4, 7, 14, 16, 20, 22, 24, 30, 31, 33, 35, 36, 39, 40, 41, 43, 46)
ON_ACT = [t not in ON_DVE for t in range(SLOTS_OF_UNIT)]


def bank(order, n):
    return (len(order) - n) % 2


class Unit:

    def __init__(self, layer, graph):
        self.layer, self.graph = layer, graph

    def before(self):
        if self.layer and isinstance(self.graph, int) and self.graph == 0:
            return Unit(0, B - 1)
        return Unit(self.layer, self.graph - 1)


class Signal:

    def __init__(self, sem, layer0, layer1=None):
        self.sem = sem
        self.per = (layer0, layer0 if layer1 is None else layer1)

    def at(self, unit, count):
        return unit.graph * self.per[unit.layer] + (unit.layer * B * self.per[0] + count)

    def begun(self, unit, count):
        value = self.at(unit, count)
        return not isinstance(value, int) or value > 0


def place(p):
    block = p // GH
    return block, block // 2, block % 2, p % GH


def two_layer_graph_attention(nc, x, adj, wq0, wk0, wv0, bv0, wo0, bo0,
                              wq1, bq1, wk1, bk1, wv1, bv1, beta, out):
    with ExitStack() as ctx:
        def sb(name, shape, dt=F32):
            return ctx.enter_context(nc.sbuf_tensor(name, [P] + shape, dt))

        def signal(name, layer0=1, layer1=None):
            return Signal(ctx.enter_context(nc.semaphore(name)), layer0, layer1)

        x1 = nc.dram_tensor("x1_scratch", [B, N, D], F32, kind="Internal").ap()

        ident = sb("ident", [P])
        raw = sb("raw", [G * D])
        adj_raw = raw[:, 0:2 * N].rearrange("p (c n) -> p c n", c=2)
        w_hi = sb("w_hi", [3, G, D], F32R)
        w_lo = sb("w_lo", [3, G, D], F32R)
        wo_hi = sb("wo_hi", [G, D], F32R)
        wo_lo = sb("wo_lo", [G, D], F32R)
        bq_col = sb("bq_col", [G])
        bk_col = sb("bk_col", [G])
        bv_row = sb("bv_row", [2, D])
        bo_row = sb("bo_row", [D])
        beta_col = sb("beta_col", [1])
        pow_col = sb("pow_col", [C])
        bias = sb("bias", [C, N])
        x_in = sb("x_in", [C, D])
        v_new = x_in
        out_rows = x_in
        spread = x_in[:].rearrange("p c d -> p (c d)").rearrange("p (g q) -> p g q", g=G)
        x_res = sb("x_res", [C, D])
        xT_hi = sb("xT_hi", [G, N], F32R)
        xT_lo = sb("xT_lo", [G, N], F32R)
        attT_hi = sb("attT_hi", [G, N], F32R)
        attT_lo = sb("attT_lo", [G, N], F32R)
        qk = sb("qk", [4, N], F32R)
        q_lo, q_hi, k_hi, k_lo = (qk[:, i, :] for i in range(4))
        stack = sb("stack", [H, 2, N], F32R)
        v_sb = sb("v_sb", [G, C, P])
        minus_s = sb("minus_s", [HELD, 2, N])
        probs = minus_s
        probsT = sb("probsT", [2, GH, C, HALF])
        minus_max = sb("minus_max", [RING, 2, GH])
        sums = sb("sums", [RING, 2, GH])
        live_row = sb("live_row", [C, H])
        rinv = sb("rinv", [C, H])
        oT = sb("oT", [G, N])
        stats = sb("stats", [C, 6])
        mean_var = sb("mean_var", [C, 2])
        var_eps = sb("var_eps", [C])
        rstd = sb("rstd", [C])

        ps_s = ctx.enter_context(nc.psum_tensor("ps_s", [P, 2, N], F32))
        ps_t = ctx.enter_context(nc.psum_tensor("ps_t", [P, TBANKS, C, P], F32))
        ps_o = ctx.enter_context(nc.psum_tensor("ps_o", [P, N], F32))
        ps_jobs = ctx.enter_context(nc.psum_tensor("ps_jobs", [P, 2, N], F32))

        setup_loaded = signal("setup_loaded")
        setup_pool = signal("setup_pool")
        setup_scaled = signal("setup_scaled")
        w_loaded = [signal(f"w_loaded{i}") for i in range(7)]
        w_hi_out, w_lo_out = signal("w_hi_out"), signal("w_lo_out")
        raw_loaded = signal("raw_loaded", 2 * DMA)
        xin_loaded = signal("xin_loaded", DMA)
        xres_loaded = signal("xres_loaded", DMA)
        stored = signal("stored", DMA)
        stacked = [signal(f"stacked{h}", 3 * DMA) for h in range(H)]
        scored = signal("scored", 2 * PAIRS)
        maxed = signal("maxed", 2 * PAIRS)
        expd = signal("expd", 2 * PAIRS)
        turned = signal("turned", 2 * PAIRS)
        turned_out_act = signal("turned_out_act", sum(ON_ACT))
        turned_out_dve = signal("turned_out_dve", 2 * PAIRS - sum(ON_ACT))
        o_ready, o_out = signal("o_ready", BLOCKS), signal("o_out", BLOCKS)
        per_job = {"x": (G, G), "q": (G, G), "k": (G, G), "v": (C, C), "n": (0, C), "r": (G, 0), "w": (C, 0)}
        job_ready = {j: signal(f"{j}_ready", *n) for j, n in per_job.items()}
        job_hi = {j: signal(f"{j}_hi_out", *per_job[j]) for j in "xqk"}
        att_hi_out, att_lo_out = signal("att_hi_out", G, 0), signal("att_lo_out", G, 0)
        summed = signal("summed", C)
        job_out = {j: signal(f"{j}_out", *per_job[j]) for j in "xqkvnr"} | {"w": summed}
        inverted = signal("inverted", BLOCKS)
        inverting = signal("inverting", 3 * BLOCKS, 0)
        spread_out = signal("spread_out", G, 0)
        bias_masked = signal("bias_masked", 0, C)
        bias_out = signal("bias_out", C)
        stats_out = signal("stats_out", C)
        mean_out = signal("mean_out", C)
        var_out = signal("var_out", 1)
        rstd_out = signal("rstd_out", 1)
        normed = signal("normed", 1)
        v_placed = signal("v_placed", G)
        bo_added = signal("bo_added", 1, 0)
        waits_carried = signal("waits_carried")

        def nodes(t, unit):
            return t[unit.graph].rearrange("(c p) d -> p c d", p=P)

        def turned_out(t):
            act = sum(ON_ACT[:t % (2 * PAIRS) + 1]) + t // (2 * PAIRS) * sum(ON_ACT)
            return (turned_out_act, act) if ON_ACT[t] else (turned_out_dve, t + 1 - act)

        def jobs_in(slot, own, post, nxt):
            jobs = SCHEDULES[0 if post is None else post.layer]
            found = []
            for n, (kind, whose, i, start) in enumerate(jobs):
                unit = {"own": own, "post": post, "next": nxt}[whose]
                if unit is not None and start <= slot < start + PARTS[kind]:
                    found.append((kind, unit, i, slot - start, bank(jobs, n)))
            return found

        def jobs_done(slot, own, post, nxt):
            return [(kind, unit, i, b) for kind, unit, i, part, b in jobs_in(slot, own, post, nxt)
                    if part == PARTS[kind] - 1]

        def first_jobs():
            return [(kind, Unit(0, 0), i, bank(FIRST_JOBS, n)) for n, (kind, i) in enumerate(FIRST_JOBS)]

        def last_jobs():
            return [("n", LAST, i, i % 2) for i in range(C)]

        def coming(slot, own, nxt):
            unit, t = (own, slot + 2 * AHEAD) if slot + 2 * AHEAD < SLOTS_OF_UNIT \
                else (nxt, slot + 2 * AHEAD - SLOTS_OF_UNIT)
            return None if unit is None else (unit, t // 2, t % 2)

        def units(eng, body):
            body(Unit(0, 0), None, Unit(0, 1))
            with eng.Fori(1, B - 1) as graph:
                body(Unit(0, graph), Unit(0, graph - 1), Unit(0, graph + 1))
            body(Unit(0, B - 1), Unit(0, B - 2), Unit(1, 0))
            body(Unit(1, 0), Unit(0, B - 1), Unit(1, 1))
            with eng.Fori(1, B - 1) as graph:
                body(Unit(1, graph), Unit(1, graph - 1), Unit(1, graph + 1))
            body(Unit(1, B - 1), Unit(1, B - 2), None)

        LAST = Unit(1, B - 1)

        def w_raw(i):
            at = probsT[:].rearrange("p b h c q -> p (b h c q)")[:, G * D * i:G * D * i + G * D] if i < 4 else raw[:]
            return at.rearrange("p (t n) -> p t n", t=G)

        weights = [(wq0, 0), (wk0, 1), (wv0, 2), (wo0, None), (wq1, 0), (wk1, 1), (wv1, 2)]
        scale = {0: float(D) ** -0.5, 4: float(HD) ** -0.5}

        block = ctx.enter_context(nc.Block())

        @block.sync
        def _(sp):
            def load_weight(i):
                if i > 4:
                    sp.wait_ge(w_lo_out.sem, i)
                sp.dma_start(w_raw(i), weights[i][0].rearrange("(t p) n -> p t n", p=P)).then_inc(w_loaded[i].sem, DMA)

            def load_adj(unit, half):
                if bias_out.begun(unit, 2 * half):
                    sp.wait_ge(bias_out.sem, bias_out.at(unit, 2 * half))
                sp.dma_start(adj_raw, nodes(adj, unit)[:, 2 * half:2 * half + 2, :]).then_inc(raw_loaded.sem, DMA)

            def load_xin(unit, own, post):
                source = x1 if unit.layer else x
                if own is not None:
                    sp.wait_ge(v_placed.sem, v_placed.at(own, G))
                if post is not None and post.layer:
                    sp.wait_ge(summed.sem, summed.at(post, C))
                elif post is not None:
                    sp.wait_ge(job_ready["r"].sem, job_ready["r"].at(post, G))
                sp.dma_start(x_in[:], nodes(source, unit)).then_inc(xin_loaded.sem, DMA)

            def load_xres(unit):
                sp.dma_start(x_res[:], nodes(x1 if unit.layer else x, unit)).then_inc(xres_loaded.sem, DMA)

            def store(post):
                sp.wait_ge(normed.sem, normed.at(post, 1))
                target = out if post.layer else x1
                sp.dma_start(nodes(target, post), x_res[:]).then_inc(stored.sem, DMA)
                sp.wait_ge(stored.sem, stored.at(post, DMA))

            def stack_group(unit, g):
                sp.wait_ge(job_out["q"].sem, job_out["q"].at(unit, g + 1))
                sp.wait_ge(job_out["k"].sem, job_out["k"].at(unit, g + 1))
                for h in range(GH):
                    for row, (first, step) in enumerate(((1, 1), (0, 2), (1, 2))):
                        sp.dma_start(stack[HD * row:HD * row + HD, GH * g + h].bitcast(F32),
                                     qk[HD * h:HD * h + HD, first:first + step + 1:step, :].bitcast(F32))\
                            .then_inc(stacked[GH * g + h].sem, DMA)

            def unit(own, post, nxt):
                stack_group(own, 1)
                if nxt is not None:
                    if nxt.layer == own.layer:
                        load_adj(nxt, 0)
                    else:
                        sp.wait_ge(bias_out.sem, bias_out.at(own, C))
                        load_weight(4)
                    load_xin(nxt, own, post)
                stack_group(own, 2)
                if nxt is not None and nxt.layer != own.layer:
                    load_weight(5)
                    load_weight(6)
                if post is not None:
                    store(post)
                    load_xres(own)
                if nxt is not None:
                    if nxt.layer != own.layer:
                        sp.wait_ge(w_lo_out.sem, 7)
                        load_adj(nxt, 0)
                    stack_group(nxt, 0)
                    load_adj(nxt, 1)

            first = Unit(0, 0)
            load_xin(first, None, None)
            for i in range(3):
                load_weight(i)
            load_adj(first, 0)
            sp.dma_start(bv_row[:, 0, :], bv0.partition_broadcast(P)).then_inc(setup_loaded.sem, DMA)
            sp.dma_start(bv_row[:, 1, :], bv1.partition_broadcast(P)).then_inc(setup_loaded.sem, DMA)
            sp.dma_start(bo_row[:], bo0.partition_broadcast(P)).then_inc(setup_loaded.sem, DMA)
            sp.dma_start(beta_col[:], beta.partition_broadcast(P)).then_inc(setup_loaded.sem, DMA)
            sp.dma_start(bq_col[:], bq1.rearrange("(g p) -> p g", p=P),
                         allow_slow_non_contiguous=True).then_inc(setup_loaded.sem, DMA)
            sp.dma_start(bk_col[:], bk1.rearrange("(g p) -> p g", p=P),
                         allow_slow_non_contiguous=True).then_inc(setup_loaded.sem, DMA)
            stack_group(first, 0)
            load_weight(3)
            load_xres(first)
            load_adj(first, 1)
            units(sp, unit)
            store(LAST)

        @block.gpsimd
        def _(pool):
            pool.memset(ident[:], 0.0).then_inc(setup_pool.sem, 1)
            pool.memset(pow_col[:], -0.5).then_inc(setup_pool.sem, 1)
            pool.wait_ge(setup_pool.sem, 2)
            pool.affine_select(out=ident[:], in_=ident[:], compare_op=ALU.not_equal, fill=1.0, base=0,
                               pattern=[[-1, P]], channel_multiplier=1).then_inc(setup_pool.sem, 1)

            def post_stage(post):
                pool.wait_ge(xres_loaded.sem, xres_loaded.at(post, DMA))
                if post.layer == 0:
                    pool.tensor_tensor(x_res[:], x_res[:], bo_row[:, None, :].to_broadcast([P, C, D]),
                                       ALU.add).then_inc(bo_added.sem, 1)
                else:
                    for c in range(C):
                        pool.wait_ge(job_out["n"].sem, job_out["n"].at(post, c + 1))
                        pool.tensor_tensor(x_res[:, c, :], out_rows[:, c, :], x_res[:, c, :],
                                           ALU.add).then_inc(summed.sem, 1)
                pool.wait_ge(var_out.sem, var_out.at(post, 1))
                pool.tensor_tensor(rstd[:], var_eps[:], pow_col[:], ALU.pow).then_inc(rstd_out.sem, 1)

            def spread_inverse(unit, g):
                pool.wait_ge(inverted.sem, inverted.at(unit, 2 * g + 2))
                at = (slice(None), slice(None), slice(GH * g, GH * g + GH), None)
                pool.tensor_tensor(spread[:, g].rearrange("p (c h d) -> p c h d", c=C, h=GH),
                                   rinv[at].to_broadcast([P, C, GH, HD]), live_row[at].to_broadcast([P, C, GH, HD]),
                                   ALU.mult).then_inc(spread_out.sem, 1)

            def place_values(unit, g):
                pool.wait_ge(job_out["v"].sem, job_out["v"].at(unit, C))
                before = unit.before()
                if o_ready.begun(before, 2 * g + 2):
                    pool.wait_ge(o_ready.sem, o_ready.at(before, 2 * g + 2))
                cols = slice(P * g, P * g + P)
                pool.tensor_tensor(v_sb[:, g], v_new[:, :, cols],
                                   bv_row[:, unit.layer, None, cols].to_broadcast([P, C, P]),
                                   ALU.add).then_inc(v_placed.sem, 1)

            def unit(own, post, nxt):
                place_values(own, 2)
                if post is not None and post.layer == 0:
                    pool.wait_ge(v_placed.sem, v_placed.at(own, G))
                    for g in range(G):
                        spread_inverse(post, g)
                if post is not None:
                    post_stage(post)
                if nxt is not None:
                    place_values(nxt, 0)
                    place_values(nxt, 1)

            pool.wait_ge(setup_loaded.sem, 6 * DMA)
            place_values(Unit(0, 0), 0)
            place_values(Unit(0, 0), 1)
            units(pool, unit)
            post_stage(LAST)

        @block.tensor
        def _(pe):
            def products(ps, a, b, part, of):
                terms = [(s, m, t) for s, m in ((a[0], b[0]), (a[0], b[1]), (a[1], b[0])) for t in range(G)]
                size = -(-len(terms) // of)
                for k, (s, m, t) in enumerate(terms):
                    if k // size == part:
                        mm = pe.matmul(ps, s(t), m(t), start=(k == 0), stop=(k == len(terms) - 1))
                return mm

            def cols(tile, *at):
                lead, (a, b) = at[:-1], at[-1]
                return lambda t: tile[(slice(None), *lead, t, slice(a, b))]

            def job(kind, unit, i, part, ps_job):
                of = PARTS[kind]
                w = w_hi, w_lo
                xT = xT_hi, xT_lo
                if kind == "x":
                    if i == 0:
                        pe.wait_ge(xin_loaded.sem, xin_loaded.at(unit, DMA))
                    for c in range(C):
                        mm = pe.transpose(ps_job[:, P * c:P * c + P], x_in[:, c, P * i:P * i + P], ident[:])
                elif kind in "qk":
                    m = "qk".index(kind)
                    pe.wait_ge(job_out["x"].sem, job_out["x"].at(unit, G))
                    pe.wait_ge(w_lo_out.sem, 4 * unit.layer + m + 1)
                    mm = products(ps_job, [cols(t, m, (P * i, P * i + P)) for t in w],
                                  [cols(t, (0, N)) for t in xT], part, of)
                elif kind == "v":
                    if i == 0 and part == 0:
                        pe.wait_ge(job_out["x"].sem, job_out["x"].at(unit, G))
                        pe.wait_ge(w_lo_out.sem, 4 * unit.layer + 3)
                    mm = products(ps_job[:, 0:D], [cols(t, (P * i, P * i + P)) for t in xT],
                                  [cols(t, 2, (0, D)) for t in w], part, of)
                elif kind == "n":
                    if i == 0:
                        pe.wait_ge(o_out.sem, o_out.at(unit, BLOCKS))
                    for g in range(G):
                        mm = pe.transpose(ps_job[:, P * g:P * g + P], oT[:, g, P * i:P * i + P], ident[:])
                elif kind == "r":
                    pe.wait_ge(spread_out.sem, spread_out.at(unit, i + 1))
                    for c in range(C):
                        mm = pe.transpose(ps_job[:, P * c:P * c + P], spread[:, i, P * c:P * c + P], ident[:])
                elif kind == "w":
                    if i == 0:
                        pe.wait_ge(w_lo_out.sem, 4)
                        pe.wait_ge(att_lo_out.sem, att_lo_out.at(unit, G))
                    mm = products(ps_job[:, 0:D], [cols(t, (P * i, P * i + P)) for t in (attT_hi, attT_lo)],
                                  [cols(t, (0, D)) for t in (wo_hi, wo_lo)], part, of)
                if part == of - 1:
                    mm.then_inc(job_ready[kind].sem, 1)

            holder = {}

            def side_job(kind, unit, i, part, bank):
                if part == 0:
                    if bank in holder:
                        before, its_unit, n = holder[bank]
                        pe.wait_ge(job_out[before].sem, job_out[before].at(its_unit, n + 1))
                    holder[bank] = kind, unit, i
                job(kind, unit, i, part, ps_jobs[:, bank])

            def score(unit, p, c):
                _, g, half, h = place(p)
                head = GH * g + h
                if half == 0 and c == 0:
                    pe.wait_ge(stacked[head].sem, stacked[head].at(unit, 3 * DMA))
                if maxed.begun(unit, 2 * p + c - 1):
                    pe.wait_ge(maxed.sem, maxed.at(unit, 2 * p + c - 1))
                q0 = P * (2 * half + c)
                pe.matmul(ps_s[:, c, :], stack[0:STACK, head, 0, q0:q0 + P],
                          stack[0:STACK, head, 1, :], start=True, stop=True).then_inc(scored.sem, 1)

            def turn(unit, p, c):
                t = 2 * p + c
                out_of_bank, count = turned_out(t - TBANKS)
                if out_of_bank.begun(unit, count):
                    pe.wait_ge(out_of_bank.sem, out_of_bank.at(unit, count))
                pe.wait_ge(expd.sem, expd.at(unit, t + 1))
                for kc in range(C):
                    mm = pe.transpose(ps_t[:, t % TBANKS, kc, :], probs[:, p % HELD, c, P * kc:P * kc + P], ident[:])
                mm.then_inc(turned.sem, 1)

            def weigh_values(unit, b, kc):
                g, half = b // 2, b % 2
                if half == 0 and kc == 0:
                    pe.wait_ge(v_placed.sem, v_placed.at(unit, g + 1))
                if kc == 0:
                    end = 2 * GH * (b + 1)
                    for t in {ON_ACT[t]: t for t in range(end - 8, end)}.values():
                        in_sbuf, count = turned_out(t)
                        pe.wait_ge(in_sbuf.sem, in_sbuf.at(unit, count))
                    if o_out.begun(unit, b):
                        pe.wait_ge(o_out.sem, o_out.at(unit, b))
                for h in range(GH):
                    mm = pe.matmul(ps_o[HD * h:HD * h + HD, HALF * half:HALF * half + HALF],
                                   v_sb[:, g, kc, HD * h:HD * h + HD], probsT[:, b % 2, h, kc, :],
                                   start=(kc == 0), stop=(kc == C - 1))
                if kc == C - 1:
                    mm.then_inc(o_ready.sem, 1)

            def unit(own, post, nxt):
                holder.update({0: ("q", own, 1), 1: ("k", own, 1)})
                for slot in range(SLOTS_OF_UNIT):
                    scoring = coming(slot, own, nxt)
                    if scoring is not None:
                        score(*scoring)
                    turn(own, slot // 2, slot % 2)
                    for kc in WEIGH_AT.get(slot % (2 * GH), ()):
                        if slot > 2 * GH:
                            weigh_values(own, slot // (2 * GH) - 1, kc)
                        elif post is not None:
                            weigh_values(post, BLOCKS - 1, kc)
                    for todo in jobs_in(slot, own, post, nxt):
                        side_job(*todo)

            pe.wait_ge(setup_pool.sem, 3)
            for kind, its_unit, i, b in first_jobs():
                for part in range(PARTS[kind]):
                    side_job(kind, its_unit, i, part, b)
            for t in range(2 * AHEAD):
                score(Unit(0, 0), t // 2, t % 2)
            units(pe, unit)
            for kc in range(C):
                weigh_values(LAST, BLOCKS - 1, kc)
            holder.clear()
            for kind, its_unit, i, b in last_jobs():
                side_job(kind, its_unit, i, 0, b)

        @block.scalar
        def _(act):
            def split_weight(i):
                m = weights[i][1]
                act.wait_ge(w_loaded[i].sem, DMA)
                if i == 4:
                    act.wait_ge(job_ready["k"].sem, job_ready["k"].at(Unit(0, B - 1), G))
                hi = wo_hi[:] if m is None else w_hi[:, m]
                act.activation(hi, w_raw(i), ACT.Copy, scale=scale.get(i, 1.0)).then_inc(w_hi_out.sem, 1)

            def job(kind, unit, i, bank):
                if kind not in "xqkv":
                    return
                ps_job = ps_jobs[:, bank]
                act.wait_ge(job_ready[kind].sem, job_ready[kind].at(unit, i + 1))
                if kind == "v":
                    if v_placed.begun(unit, 0):
                        act.wait_ge(v_placed.sem, v_placed.at(unit, 0))
                    act.activation(v_new[:, i, :], ps_job[:, 0:D], ACT.Copy).then_inc(job_out["v"].sem, 1)
                    return
                if kind in "qk":
                    before, g = (unit, i - 1) if i else (unit.before(), G - 1)
                    for head in range(GH * g, GH * g + GH):
                        if stacked[head].begun(before, 3 * DMA):
                            act.wait_ge(stacked[head].sem, stacked[head].at(before, 3 * DMA))
                to = {"x": xT_hi[:, i, :], "q": q_hi, "k": k_hi}[kind]
                if kind in "qk" and unit.layer:
                    col = (bq_col if kind == "q" else bk_col)[:, i:i + 1]
                    done = act.activation(to, ps_job, ACT.Identity, bias=col)
                else:
                    done = act.activation(to, ps_job, ACT.Copy)
                done.then_inc(job_hi[kind].sem, 1)

            def att_hi_part(unit, g):
                act.wait_ge(job_out["r"].sem, job_out["r"].at(unit, g + 1))
                act.activation(attT_hi[:, g, :], oT[:, g, :], ACT.Copy).then_inc(att_hi_out.sem, 1)

            def exponentials(unit, p, c):
                b, _, _, h = place(p)
                if p % GH == 0 and c == 0:
                    if inverted.begun(unit, b - RING + 1):
                        act.wait_ge(inverted.sem, inverted.at(unit, b - RING + 1))
                act.wait_ge(maxed.sem, maxed.at(unit, 2 * p + c + 1))
                act.activation(probs[:, p % HELD, c, :], minus_s[:, p % HELD, c, :], ACT.Exp,
                               bias=minus_max[:, b % RING, c, h:h + 1], scale=-1.0,
                               accum_out=sums[:, b % RING, c, h:h + 1]).then_inc(expd.sem, 1)

            def turned_copy(unit, t):
                b, _, _, h = place(t // 2)
                c = t % 2
                if o_ready.begun(unit, b - 1):
                    act.wait_ge(o_ready.sem, o_ready.at(unit, b - 1))
                act.wait_ge(turned.sem, turned.at(unit, t + 1))
                act.activation(probsT[:, b % 2, h, :, P * c:P * c + P], ps_t[:, t % TBANKS],
                               ACT.Copy).then_inc(turned_out_act.sem, 1)

            def o_copy(unit, b):
                g, half = b // 2, b % 2
                before = unit.before()
                act.wait_ge(o_ready.sem, o_ready.at(unit, b + 1))
                if before.layer and g == 0:
                    act.wait_ge(job_ready["n"].sem, job_ready["n"].at(before, 2 * half + 2))
                elif not before.layer and half == 0 and att_lo_out.begun(before, g + 1):
                    act.wait_ge(att_lo_out.sem, att_lo_out.at(before, g + 1))
                cols = slice(HALF * half, HALF * half + HALF)
                act.activation(oT[:, g, cols], ps_o[:, cols], ACT.Copy).then_inc(o_out.sem, 1)

            def unit(own, post, nxt):
                for slot in range(SLOTS_OF_UNIT):
                    if slot:
                        for todo in jobs_done(slot - 1, own, post, nxt):
                            job(*todo)
                    if slot > 1:
                        for kind, its_unit, i, _ in jobs_done(slot - 2, own, post, nxt):
                            if kind == "r":
                                att_hi_part(its_unit, i)
                    if slot % (2 * GH) == O_COPY_AT:
                        if slot > 2 * GH:
                            o_copy(own, slot // (2 * GH) - 1)
                        elif post is not None:
                            o_copy(post, BLOCKS - 1)
                    if ON_ACT[slot]:
                        turned_copy(own, slot)
                    scoring = coming(slot, own, nxt)
                    if scoring is not None:
                        exponentials(*scoring)
                    if nxt is not None and nxt.layer != own.layer and slot in WEIGHT_SLOTS:
                        split_weight(4 + WEIGHT_SLOTS.index(slot))

            for todo in first_jobs()[:G]:
                job(*todo)
            for i in range(3):
                split_weight(i)
            for todo in first_jobs()[G:-2]:
                job(*todo)
            for t in range(2 * AHEAD):
                exponentials(Unit(0, 0), t // 2, t % 2)
            for todo in first_jobs()[-2:]:
                job(*todo)
            split_weight(3)
            act.wait_ge(setup_scaled.sem, 1)
            units(act, unit)
            o_copy(LAST, BLOCKS - 1)

        @block.vector
        def _(dve):
            def carry_wait():
                dve.sem_inc(waits_carried.sem, 1)

            def split_weight(i):
                m = weights[i][1]
                dve.wait_ge(w_hi_out.sem, i + 1)
                hi, lo = (wo_hi[:], wo_lo[:]) if m is None else (w_hi[:, m], w_lo[:, m])
                flat = "p t n -> p (t n)"
                dve.scalar_tensor_tensor(lo.rearrange(flat), w_raw(i).rearrange(flat), scale.get(i, 1.0),
                                         hi.bitcast(F32).rearrange(flat), ALU.mult,
                                         ALU.subtract).then_inc(w_lo_out.sem, 1)

            def make_bias(unit, c):
                raw_rows, to = adj_raw[:, c % 2, :], bias[:, c, :]
                before, last = unit.before(), 2 * GH * (BLOCKS - 1 + c // 2) - 1 + c % 2
                if maxed.begun(before, last):
                    dve.wait_ge(maxed.sem, maxed.at(before, last))
                if c % 2 == 0:
                    dve.wait_ge(raw_loaded.sem, raw_loaded.at(unit, DMA * (c // 2 + 1)))
                if unit.layer == 0:
                    dve.tensor_scalar(to, raw_rows, 2.0, None, ALU.mult).then_inc(bias_out.sem, 1)
                else:
                    dve.tensor_scalar(to, raw_rows, 0.0, MASKED, ALU.is_le, ALU.mult).then_inc(bias_masked.sem, 1)
                    dve.wait_ge(bias_masked.sem, bias_masked.at(unit, c + 1))
                    dve.scalar_tensor_tensor(to, raw_rows, beta_col[:, 0:1], to, ALU.mult,
                                             ALU.add).then_inc(bias_out.sem, 1)

            def maxima(unit, p, c):
                b, g, half, h = place(p)
                if h == 0 and g == 0:
                    dve.wait_ge(bias_out.sem, bias_out.at(unit, 2 * half + c + 1))
                dve.wait_ge(scored.sem, scored.at(unit, 2 * p + c + 1))
                carry_wait()
                dve.tensor_tensor_reduce(minus_s[:, p % HELD, c, :], ps_s[:, c, :], bias[:, 2 * half + c, :],
                                         -1.0, BIG, ALU.add, ALU.min,
                                         minus_max[:, b % RING, c, h:h + 1]).then_inc(maxed.sem, 1)

            def invert(unit, b):
                g, half = b // 2, b % 2
                at = (slice(None), slice(2 * half, 2 * half + 2), slice(GH * g, GH * g + GH))
                dve.wait_ge(expd.sem, expd.at(unit, 2 * GH * (b + 1)))
                s, m = sums[:, b % RING], minus_max[:, b % RING]
                if unit.layer:
                    dve.reciprocal(rinv[at], s).then_inc(inverted.sem, 1)
                    return
                dve.reciprocal(rinv[at], s).then_inc(inverting.sem, 1)
                dve.tensor_scalar(live_row[at], s, float(N), None, ALU.is_equal).then_inc(inverting.sem, 1)
                dve.wait_ge(inverting.sem, inverting.at(unit, 3 * b + 2))
                dve.scalar_tensor_tensor(live_row[at], m, 0.0, live_row[at], ALU.is_equal,
                                         ALU.mult).then_inc(inverting.sem, 1)
                dve.wait_ge(inverting.sem, inverting.at(unit, 3 * b + 3))
                dve.tensor_scalar(live_row[at], live_row[at], -1.0, 1.0, ALU.mult, ALU.add)\
                    .then_inc(inverted.sem, 1)

            def turned_copy(unit, t):
                b, _, _, h = place(t // 2)
                c = t % 2
                if o_ready.begun(unit, b - 1):
                    dve.wait_ge(o_ready.sem, o_ready.at(unit, b - 1))
                dve.wait_ge(turned.sem, turned.at(unit, t + 1))
                dve.tensor_copy(probsT[:, b % 2, h, :, P * c:P * c + P],
                                ps_t[:, t % TBANKS]).then_inc(turned_out_dve.sem, 1)

            def row_stats(unit, c):
                dve.wait_ge(summed.sem, summed.at(unit, c + 1))
                dve.bn_stats(stats[:, c, :], x_res[:, c, :]).then_inc(stats_out.sem, 1)

            def job(kind, unit, i, bank):
                if kind == "v":
                    return
                ps_job = ps_jobs[:, bank]
                if kind in job_hi:
                    dve.wait_ge(job_hi[kind].sem, job_hi[kind].at(unit, i + 1))
                    if kind == "x":
                        hi, lo = xT_hi[:, i, :], xT_lo[:, i, :]
                    else:
                        hi, lo = (q_hi, q_lo) if kind == "q" else (k_hi, k_lo)
                    if kind in "qk" and unit.layer:
                        col = (bq_col if kind == "q" else bk_col)[:, i:i + 1]
                        done = dve.scalar_tensor_tensor(lo, ps_job, col, hi.bitcast(F32), ALU.add, ALU.subtract)
                    else:
                        done = dve.tensor_tensor(lo, ps_job, hi.bitcast(F32), ALU.subtract)
                    done.then_inc(job_out[kind].sem, 1)
                    return
                dve.wait_ge(job_ready[kind].sem, job_ready[kind].at(unit, i + 1))
                if kind == "n":
                    if i == 0:
                        dve.wait_ge(inverted.sem, inverted.at(unit, BLOCKS))
                        dve.wait_ge(v_placed.sem, v_placed.at(unit, G if unit is LAST else 2 * G))
                    dve.tensor_tensor(out_rows[:, i, :].rearrange("p (h d) -> p h d", h=H),
                                      ps_job[:, 0:D].rearrange("p (h d) -> p h d", h=H),
                                      rinv[:, i, :, None].to_broadcast([P, H, HD]),
                                      ALU.mult).then_inc(job_out["n"].sem, 1)
                    if i:
                        row_stats(unit, i - 1)
                elif kind == "r":
                    if i == G - 1:
                        dve.wait_ge(o_out.sem, o_out.at(unit, BLOCKS))
                    dve.tensor_tensor(oT[:, i, :], ps_job, oT[:, i, :], ALU.mult).then_inc(job_out["r"].sem, 1)
                elif kind == "w":
                    if i == 0:
                        dve.wait_ge(bo_added.sem, bo_added.at(unit, 1))
                    dve.tensor_tensor(x_res[:, i, :], ps_job[:, 0:D], x_res[:, i, :], ALU.add)\
                        .then_inc(summed.sem, 1)
                    row_stats(unit, i)

            def att_lo_part(unit, g):
                dve.wait_ge(att_hi_out.sem, att_hi_out.at(unit, g + 1))
                dve.tensor_tensor(attT_lo[:, g, :], oT[:, g, :], attT_hi[:, g, :].bitcast(F32),
                                  ALU.subtract).then_inc(att_lo_out.sem, 1)

            def layer_norm_mean(unit):
                if unit.layer:
                    row_stats(unit, C - 1)
                for c in range(C):
                    if c == 0:
                        dve.wait_ge(stats_out.sem, stats_out.at(unit, C))
                        carry_wait()
                    dve.bn_aggr(mean_var[:, c, :], stats[:, c, :]).then_inc(mean_out.sem, 1)
                dve.wait_ge(mean_out.sem, mean_out.at(unit, C))
                dve.tensor_scalar(var_eps[:], mean_var[:, :, 1], LN_EPS, None, ALU.add).then_inc(var_out.sem, 1)

            def layer_norm(unit):
                dve.wait_ge(rstd_out.sem, rstd_out.at(unit, 1))
                for c in range(C):
                    done = dve.tensor_scalar(x_res[:, c, :], x_res[:, c, :], mean_var[:, c, 0:1], rstd[:, c:c + 1],
                                             ALU.subtract, ALU.mult)
                done.then_inc(normed.sem, 1)

            def unit(own, post, nxt):
                for slot in range(SLOTS_OF_UNIT):
                    if slot % (2 * GH) == C:
                        if slot > 2 * GH:
                            invert(own, slot // (2 * GH) - 1)
                        elif post is not None:
                            invert(post, BLOCKS - 1)
                    scoring = coming(slot, own, nxt)
                    if scoring is not None:
                        maxima(*scoring)
                    if not ON_ACT[slot]:
                        turned_copy(own, slot)
                    if slot:
                        for todo in jobs_done(slot - 1, own, post, nxt):
                            job(*todo)
                    if slot > 1:
                        for kind, its_unit, i, _ in jobs_done(slot - 2, own, post, nxt):
                            if kind == "r":
                                att_lo_part(its_unit, i)
                    if post is not None:
                        if slot == NORM_SLOT[post.layer]:
                            layer_norm_mean(post)
                        if slot == NORMED_SLOT[post.layer]:
                            layer_norm(post)
                    if nxt is not None:
                        if slot in BIAS_SLOTS:
                            make_bias(nxt, BIAS_SLOTS.index(slot))
                        if nxt.layer != own.layer and slot in WEIGHT_SLOTS:
                            split_weight(4 + WEIGHT_SLOTS.index(slot))

            for todo in first_jobs()[:G]:
                job(*todo)
            for i in range(3):
                split_weight(i)
            for todo in first_jobs()[G:-2]:
                job(*todo)
            for c in range(2):
                make_bias(Unit(0, 0), c)
            for t in range(2 * AHEAD):
                maxima(Unit(0, 0), t // 2, t % 2)
            for todo in first_jobs()[-2:]:
                job(*todo)
            for c in range(2, C):
                make_bias(Unit(0, 0), c)
            split_weight(3)
            dve.wait_ge(setup_loaded.sem, 6 * DMA)
            dve.tensor_scalar(bq_col[:], bq_col[:], scale[4], None, ALU.mult).then_inc(setup_scaled.sem, 1)
            units(dve, unit)
            invert(LAST, BLOCKS - 1)
            for todo in last_jobs():
                job(*todo)
            layer_norm_mean(LAST)
            layer_norm(LAST)


_INS = ["x", "adj", "L0_gnn_Wq", "L0_gnn_Wk", "L0_gnn_Wv", "L0_gnn_bv", "L0_gnn_Wo", "L0_gnn_bo",
        "L1_gnn_Wq", "L1_gnn_bq", "L1_gnn_Wk", "L1_gnn_bk", "L1_gnn_Wv", "L1_gnn_bv", "L1_gnn_beta"]
_TRANSPOSED = ("L0_gnn_Wq", "L0_gnn_Wk", "L0_gnn_Wv", "L0_gnn_Wo")


def kernel(**inputs):
    import numpy as _np
    import concourse.bacc as _bacc
    from concourse import mybir as _mybir
    from concourse.bass_utils import run_bass_kernel_spmd as _run

    nc = _bacc.Bacc("TRN2", target_bir_lowering=False, num_devices=1)
    arrays, args = {}, []
    for name in _INS:
        a = _np.asarray(inputs[name])
        if name in _TRANSPOSED:
            a = a.T
        a = _np.ascontiguousarray(a.reshape(1) if a.ndim == 0 else a)
        arrays[f"in_{name}_dram"] = a
        args.append(nc.dram_tensor(f"in_{name}_dram", a.shape, _mybir.dt.from_np(a.dtype), kind="ExternalInput").ap())
    o = nc.dram_tensor("out_0_dram", (B, N, D), F32, kind="ExternalOutput").ap()
    two_layer_graph_attention(nc, *args, o)
    r = _run(nc, [arrays], core_ids=[0])
    return r.results[0]["out_0_dram"]
```
